# Optimizing a Trainium2 kernel written in Bass

```python
import numpy as np
import jax
import jax.numpy as jnp

def _softmax(x, axis=-1):
    return jax.nn.softmax(x, axis=axis)

def _gelu(x):
    return jax.nn.gelu(x, approximate=True)

def _silu(x):
    return jax.nn.silu(x)

def _sigmoid(x):
    return jax.nn.sigmoid(x)

def _layernorm(x, axis=-1, eps=1e-05):
    m = jnp.mean(x, axis=axis, keepdims=True)
    v = jnp.var(x, axis=axis, keepdims=True)
    return (x - m) / jnp.sqrt(v + eps)

def _scatter_add(tgt, idx, src, axis=0):
    return tgt.at[idx].add(src)

def _segment_sum(src, seg, n):
    return jax.ops.segment_sum(src, seg, n)
kernel_name = 'mk_decoder_postln_d1_seqx_r8_6b1dbd'

def setup_inputs(seed: int=0):
    np.random.seed(seed)
    _w = jnp.asarray

    def _rec_inputs():
        import jax
        import jax.numpy as jnp
        _rk = jax.random.key(seed)
        x = 7.22e-05 + 1 * jax.random.normal(jax.random.fold_in(_rk, 1), (128, 64, 128), jnp.float32)
        _lenS = 64 - jax.random.randint(jax.random.fold_in(_rk, 7), (128,), 0, max(1, 64 // 4) + 1, jnp.int32)
        _lenS2 = 64 - jax.random.randint(jax.random.fold_in(_rk, 8), (128,), 0, max(1, 64 // 4) + 1, jnp.int32)
        _ctx_1024P = jax.random.normal(jax.random.fold_in(_rk, 11), (128, 16, 128), jnp.float32)
        _ctx_1024c = jax.random.dirichlet(jax.random.fold_in(_rk, 511), 0.3 * jnp.ones((16,), jnp.float32), (128, 64))
        _ctx_1024t = jnp.einsum('bsk,bkd->bsd', _ctx_1024c, _ctx_1024P)
        _ctx_1024t = _ctx_1024t * jax.lax.rsqrt(jnp.mean(jnp.square(_ctx_1024t)) + 1e-12) * 0.953939
        ctx_1024 = 4.13588e-05 + 0.999923 * (_ctx_1024t + 0.3 * jax.random.normal(jax.random.fold_in(_rk, 611), (128, 64, 128), jnp.float32))
        return (x, ctx_1024)
    x, ctx_1024 = _rec_inputs()

    def _L0_attn_setup():
        import jax, jax.numpy as jnp
        import numpy as np
        from jax import lax
        D_MODEL = 128
        D_STATE = 16
        D_CONV = 4
        EXPAND = 2
        D_INNER = EXPAND * D_MODEL
        DT_RANK = -(-D_MODEL // 16)
        BATCH = 2
        T = 128

        def _silu(u):
            return u * jax.nn.sigmoid(u)

        def _forward(x, W_in, conv_w, conv_b, W_xproj, W_dt, b_dt, A_log, D_param, W_out):
            B, Tlen, _ = x.shape
            xz = x @ W_in
            x_b, z = jnp.split(xz, 2, axis=-1)
            xpad = jnp.pad(x_b, ((0, 0), (D_CONV - 1, 0), (0, 0)))
            xc = conv_b
            for k in range(D_CONV):
                xc = xc + xpad[:, k:k + Tlen, :] * conv_w[:, k]
            xc = _silu(xc)
            proj = xc @ W_xproj
            delta_raw = proj[..., :DT_RANK]
            B_in = proj[..., DT_RANK:DT_RANK + D_STATE]
            C_in = proj[..., DT_RANK + D_STATE:]
            delta = jax.nn.softplus(delta_raw @ W_dt + b_dt)
            A = -jnp.exp(A_log)
            A_bar = jnp.exp(delta[..., None] * A)
            Bx = delta[..., None] * B_in[:, :, None, :] * xc[..., None]

            def step(h, ins):
                a_t, bx_t, c_t, xc_t = ins
                h = a_t * h + bx_t
                y_t = jnp.einsum('bds,bs->bd', h, c_t) + D_param * xc_t
                return (h, y_t)
            h0 = jnp.zeros((B, D_INNER, D_STATE), dtype=x.dtype)
            ins = (jnp.swapaxes(A_bar, 0, 1), jnp.swapaxes(Bx, 0, 1), jnp.swapaxes(C_in, 0, 1), jnp.swapaxes(xc, 0, 1))
            _, ys = lax.scan(step, h0, ins)
            y = jnp.swapaxes(ys, 0, 1) * _silu(z)
            return y @ W_out
        key = jax.random.key(seed)
        ks = jax.random.split(key, 9)
        s = 0.02
        x = jax.random.normal(ks[0], (BATCH, T, D_MODEL), dtype=jnp.float32)
        W_in = jax.random.normal(ks[1], (D_MODEL, 2 * D_INNER), dtype=jnp.float32) * s
        conv_w = jax.random.normal(ks[2], (D_INNER, D_CONV), dtype=jnp.float32) * 0.2
        conv_b = jax.random.normal(ks[3], (D_INNER,), dtype=jnp.float32) * 0.02
        W_xproj = jax.random.normal(ks[4], (D_INNER, DT_RANK + 2 * D_STATE), dtype=jnp.float32) * s
        W_dt = jax.random.normal(ks[5], (DT_RANK, D_INNER), dtype=jnp.float32) * s
        b_dt = jax.random.normal(ks[6], (D_INNER,), dtype=jnp.float32) * 0.02
        A_log = jnp.broadcast_to(jnp.log(jnp.arange(1, D_STATE + 1, dtype=jnp.float32)), (D_INNER, D_STATE)).copy()
        D_param = jnp.ones((D_INNER,), dtype=jnp.float32)
        W_out = jax.random.normal(ks[7], (D_INNER, D_MODEL), dtype=jnp.float32) * s
        return {'x': x, 'W_in': W_in, 'conv_w': conv_w, 'conv_b': conv_b, 'W_xproj': W_xproj, 'W_dt': W_dt, 'b_dt': b_dt, 'A_log': A_log, 'D_param': D_param, 'W_out': W_out}
    _L0_attn_all = _L0_attn_setup()
    _L0_attn_in = {k: v for k, v in _L0_attn_all.items() if k in ('W_in', 'conv_w', 'conv_b', 'W_xproj', 'W_dt', 'b_dt', 'A_log', 'D_param', 'W_out')}
    del _L0_attn_all

    def _L0_xattn_setup():
        import jax, jax.numpy as jnp
        import numpy as np
        THETA = 10000.0
        SCALE_BASE = 512.0
        GAMMA = 0.96875

        def _dup_interleave(x):
            return jnp.repeat(x, 2, axis=-1)

        def _xpos(x, offset, inverse_scale):
            L, d = (x.shape[-2], x.shape[-1])
            half = d // 2
            base = (jnp.arange(0, d, 2, dtype=x.dtype) + 0.4 * d) / (1.4 * d)
            pos = jnp.arange(offset, offset + L, dtype=x.dtype)
            scale = base[None, :] ** (pos[:, None] / SCALE_BASE)
            freqs = 1.0 / THETA ** (jnp.arange(half, dtype=x.dtype) / half)
            sin_in = pos[:, None] * freqs[None, :]
            if inverse_scale:
                scale = 1.0 / scale
            sin = _dup_interleave(jnp.sin(sin_in) * scale)
            cos = _dup_interleave(jnp.cos(sin_in) * scale)
            rot = jnp.stack((-x[..., 1::2], x[..., ::2]), axis=-1).reshape(x.shape)
            return x * cos + rot * sin

        def _decay_mask(L, gamma, dtype):
            u = jnp.arange(L, dtype=dtype)[:, None]
            v = jnp.arange(L, dtype=dtype)[None, :]
            return jnp.where(u >= v, gamma ** (u - v), jnp.zeros((), dtype))
        key = jax.random.key(seed)
        ks = jax.random.split(key, 6)
        B, L, E = (2, 512, 128)
        query = jax.random.normal(ks[0], (B, L, E), jnp.float32)
        k_in = jax.random.normal(ks[1], (B, L, E), jnp.float32)
        value = jax.random.normal(ks[2], (B, L, E), jnp.float32)
        s = 1.0 / np.sqrt(E)
        Wq = jax.random.normal(ks[3], (E, E), jnp.float32) * s
        Wk = jax.random.normal(ks[4], (E, E), jnp.float32) * s
        Wv = jax.random.normal(ks[5], (E, E), jnp.float32) * s
        return {'query': query, 'key': k_in, 'value': value, 'Wq': Wq, 'Wk': Wk, 'Wv': Wv}
    _L0_xattn_all = _L0_xattn_setup()
    _L0_xattn_in = {k: v for k, v in _L0_xattn_all.items() if k in ('Wq', 'Wk', 'Wv')}
    del _L0_xattn_all

    def _L0_ffn_setup():
        import jax, jax.numpy as jnp
        import numpy as np
        DIM = 128
        EXPERT_DIM = 64
        N_EXPERTS = 16
        TOPK = 2
        SHARED_HIDDEN = EXPERT_DIM * TOPK
        B, T = (4, 128)

        def _moe_forward(x, router_w, router_bias, up_proj, gate_proj, down_proj, sh_gate, sh_up, sh_down):
            Bb, Tt, D = x.shape
            flat = x.reshape(Bb * Tt, D)
            N = flat.shape[0]
            logits = flat @ router_w.T
            topk_scores, topk_idx = jax.lax.top_k(logits + router_bias, TOPK)
            topk_scores = jax.nn.softmax(topk_scores, axis=-1)
            combine = jnp.zeros((N, N_EXPERTS), flat.dtype)
            combine = combine.at[jnp.arange(N)[:, None], topk_idx].add(topk_scores)
            up_all = jnp.einsum('nd,kde->nke', flat, up_proj)
            gate_all = jnp.einsum('nd,kde->nke', flat, gate_proj)
            hidden = jax.nn.silu(gate_all) * up_all
            down_all = jnp.einsum('nke,ked->nkd', hidden, down_proj)
            out = jnp.einsum('nk,nkd->nd', combine, down_all)
            sh_hidden = jax.nn.silu(flat @ sh_gate.T) * (flat @ sh_up.T)
            out = out + sh_hidden @ sh_down.T
            return out.reshape(Bb, Tt, D)
        key = jax.random.key(seed)
        ks = jax.random.split(key, 9)
        std = 0.02
        return {'x': jax.random.normal(ks[0], (B, T, DIM), jnp.float32), 'router_w': jax.random.normal(ks[1], (N_EXPERTS, DIM), jnp.float32) * std, 'router_bias': jnp.zeros((N_EXPERTS,), jnp.float32), 'up_proj': jax.random.normal(ks[2], (N_EXPERTS, DIM, EXPERT_DIM), jnp.float32) * std, 'gate_proj': jax.random.normal(ks[3], (N_EXPERTS, DIM, EXPERT_DIM), jnp.float32) * std, 'down_proj': jax.random.normal(ks[4], (N_EXPERTS, EXPERT_DIM, DIM), jnp.float32) * std, 'sh_gate': jax.random.normal(ks[5], (SHARED_HIDDEN, DIM), jnp.float32) * std, 'sh_up': jax.random.normal(ks[6], (SHARED_HIDDEN, DIM), jnp.float32) * std, 'sh_down': jax.random.normal(ks[7], (DIM, SHARED_HIDDEN), jnp.float32) * std}
    _L0_ffn_all = _L0_ffn_setup()
    _L0_ffn_in = {k: v for k, v in _L0_ffn_all.items() if k in ('router_w', 'router_bias', 'up_proj', 'gate_proj', 'down_proj', 'sh_gate', 'sh_up', 'sh_down')}
    del _L0_ffn_all
    return {'x': x, 'ctx_1024': ctx_1024, 'L0_attn_W_in': _L0_attn_in['W_in'], 'L0_attn_conv_w': _L0_attn_in['conv_w'], 'L0_attn_conv_b': _L0_attn_in['conv_b'], 'L0_attn_W_xproj': _L0_attn_in['W_xproj'], 'L0_attn_W_dt': _L0_attn_in['W_dt'], 'L0_attn_b_dt': _L0_attn_in['b_dt'], 'L0_attn_A_log': _L0_attn_in['A_log'], 'L0_attn_D_param': _L0_attn_in['D_param'], 'L0_attn_W_out': _L0_attn_in['W_out'], 'L0_xattn_Wq': _L0_xattn_in['Wq'], 'L0_xattn_Wk': _L0_xattn_in['Wk'], 'L0_xattn_Wv': _L0_xattn_in['Wv'], 'L0_ffn_router_w': _L0_ffn_in['router_w'], 'L0_ffn_router_bias': _L0_ffn_in['router_bias'], 'L0_ffn_up_proj': _L0_ffn_in['up_proj'], 'L0_ffn_gate_proj': _L0_ffn_in['gate_proj'], 'L0_ffn_down_proj': _L0_ffn_in['down_proj'], 'L0_ffn_sh_gate': _L0_ffn_in['sh_gate'], 'L0_ffn_sh_up': _L0_ffn_in['sh_up'], 'L0_ffn_sh_down': _L0_ffn_in['sh_down']}

def reference(x, ctx_1024, L0_attn_W_in, L0_attn_conv_w, L0_attn_conv_b, L0_attn_W_xproj, L0_attn_W_dt, L0_attn_b_dt, L0_attn_A_log, L0_attn_D_param, L0_attn_W_out, L0_xattn_Wq, L0_xattn_Wk, L0_xattn_Wv, L0_ffn_router_w, L0_ffn_router_bias, L0_ffn_up_proj, L0_ffn_gate_proj, L0_ffn_down_proj, L0_ffn_sh_gate, L0_ffn_sh_up, L0_ffn_sh_down):
    import jax
    import jax.numpy as jnp

    def _L0_attn_ref(x, W_in, conv_w, conv_b, W_xproj, W_dt, b_dt, A_log, D_param, W_out):
        import jax, jax.numpy as jnp
        import numpy as np
        from jax import lax
        D_MODEL = 128
        D_STATE = 16
        D_CONV = 4
        EXPAND = 2
        D_INNER = EXPAND * D_MODEL
        DT_RANK = -(-D_MODEL // 16)
        BATCH = 2
        T = 128

        def _silu(u):
            return u * jax.nn.sigmoid(u)

        def _forward(x, W_in, conv_w, conv_b, W_xproj, W_dt, b_dt, A_log, D_param, W_out):
            B, Tlen, _ = x.shape
            xz = x @ W_in
            x_b, z = jnp.split(xz, 2, axis=-1)
            xpad = jnp.pad(x_b, ((0, 0), (D_CONV - 1, 0), (0, 0)))
            xc = conv_b
            for k in range(D_CONV):
                xc = xc + xpad[:, k:k + Tlen, :] * conv_w[:, k]
            xc = _silu(xc)
            proj = xc @ W_xproj
            delta_raw = proj[..., :DT_RANK]
            B_in = proj[..., DT_RANK:DT_RANK + D_STATE]
            C_in = proj[..., DT_RANK + D_STATE:]
            delta = jax.nn.softplus(delta_raw @ W_dt + b_dt)
            A = -jnp.exp(A_log)
            A_bar = jnp.exp(delta[..., None] * A)
            Bx = delta[..., None] * B_in[:, :, None, :] * xc[..., None]

            def step(h, ins):
                a_t, bx_t, c_t, xc_t = ins
                h = a_t * h + bx_t
                y_t = jnp.einsum('bds,bs->bd', h, c_t) + D_param * xc_t
                return (h, y_t)
            h0 = jnp.zeros((B, D_INNER, D_STATE), dtype=x.dtype)
            ins = (jnp.swapaxes(A_bar, 0, 1), jnp.swapaxes(Bx, 0, 1), jnp.swapaxes(C_in, 0, 1), jnp.swapaxes(xc, 0, 1))
            _, ys = lax.scan(step, h0, ins)
            y = jnp.swapaxes(ys, 0, 1) * _silu(z)
            return y @ W_out
        return _forward(x, W_in, conv_w, conv_b, W_xproj, W_dt, b_dt, A_log, D_param, W_out)

    def _L0_xattn_ref(query, key, value, Wq, Wk, Wv):
        import jax, jax.numpy as jnp
        import numpy as np
        THETA = 10000.0
        SCALE_BASE = 512.0
        GAMMA = 0.96875

        def _dup_interleave(x):
            return jnp.repeat(x, 2, axis=-1)

        def _xpos(x, offset, inverse_scale):
            L, d = (x.shape[-2], x.shape[-1])
            half = d // 2
            base = (jnp.arange(0, d, 2, dtype=x.dtype) + 0.4 * d) / (1.4 * d)
            pos = jnp.arange(offset, offset + L, dtype=x.dtype)
            scale = base[None, :] ** (pos[:, None] / SCALE_BASE)
            freqs = 1.0 / THETA ** (jnp.arange(half, dtype=x.dtype) / half)
            sin_in = pos[:, None] * freqs[None, :]
            if inverse_scale:
                scale = 1.0 / scale
            sin = _dup_interleave(jnp.sin(sin_in) * scale)
            cos = _dup_interleave(jnp.cos(sin_in) * scale)
            rot = jnp.stack((-x[..., 1::2], x[..., ::2]), axis=-1).reshape(x.shape)
            return x * cos + rot * sin

        def _decay_mask(L, gamma, dtype):
            u = jnp.arange(L, dtype=dtype)[:, None]
            v = jnp.arange(L, dtype=dtype)[None, :]
            return jnp.where(u >= v, gamma ** (u - v), jnp.zeros((), dtype))
        q = jnp.einsum('ble,de->bld', query, Wq)
        k = jnp.einsum('ble,de->bld', key, Wk)
        v = jnp.einsum('ble,de->bld', value, Wv)
        q = _xpos(q, 0, False)
        k = _xpos(k, 0, True)
        L = q.shape[-2]
        mask = _decay_mask(L, jnp.asarray(GAMMA, q.dtype), q.dtype)
        retention = jnp.einsum('bqd,bkd->bqk', q, k) * mask[None, :, :]
        out = jnp.einsum('bqk,bkv->bqv', retention, v)
        return out

    def _L0_ffn_ref(x, router_w, router_bias, up_proj, gate_proj, down_proj, sh_gate, sh_up, sh_down):
        import jax, jax.numpy as jnp
        import numpy as np
        DIM = 128
        EXPERT_DIM = 64
        N_EXPERTS = 16
        TOPK = 2
        SHARED_HIDDEN = EXPERT_DIM * TOPK
        B, T = (4, 128)

        def _moe_forward(x, router_w, router_bias, up_proj, gate_proj, down_proj, sh_gate, sh_up, sh_down):
            Bb, Tt, D = x.shape
            flat = x.reshape(Bb * Tt, D)
            N = flat.shape[0]
            logits = flat @ router_w.T
            topk_scores, topk_idx = jax.lax.top_k(logits + router_bias, TOPK)
            topk_scores = jax.nn.softmax(topk_scores, axis=-1)
            combine = jnp.zeros((N, N_EXPERTS), flat.dtype)
            combine = combine.at[jnp.arange(N)[:, None], topk_idx].add(topk_scores)
            up_all = jnp.einsum('nd,kde->nke', flat, up_proj)
            gate_all = jnp.einsum('nd,kde->nke', flat, gate_proj)
            hidden = jax.nn.silu(gate_all) * up_all
            down_all = jnp.einsum('nke,ked->nkd', hidden, down_proj)
            out = jnp.einsum('nk,nkd->nd', combine, down_all)
            sh_hidden = jax.nn.silu(flat @ sh_gate.T) * (flat @ sh_up.T)
            out = out + sh_hidden @ sh_down.T
            return out.reshape(Bb, Tt, D)
        return _moe_forward(x, router_w, router_bias, up_proj, gate_proj, down_proj, sh_gate, sh_up, sh_down)
    x = _layernorm(x + _L0_attn_ref(x, L0_attn_W_in, L0_attn_conv_w, L0_attn_conv_b, L0_attn_W_xproj, L0_attn_W_dt, L0_attn_b_dt, L0_attn_A_log, L0_attn_D_param, L0_attn_W_out), axis=-1)
    x = _layernorm(x + _L0_xattn_ref(x, ctx_1024, ctx_1024, L0_xattn_Wq, L0_xattn_Wk, L0_xattn_Wv), axis=-1)
    x = _layernorm(x + _L0_ffn_ref(x, L0_ffn_router_w, L0_ffn_router_bias, L0_ffn_up_proj, L0_ffn_gate_proj, L0_ffn_down_proj, L0_ffn_sh_gate, L0_ffn_sh_up, L0_ffn_sh_down), axis=-1)
    return x

_drawn_inputs = setup_inputs


def setup_inputs(seed=0):
    import zlib

    import numpy as np

    out = dict(_drawn_inputs(seed))
    spreads = {'L0_attn_D_param': (1.0, 0.6), 'L0_ffn_router_bias': (0.0, 0.8)}
    factors = {'L0_attn_W_in': 8.0,
     'L0_attn_conv_w': 8.0,
     'L0_attn_conv_b': 8.0,
     'L0_attn_W_xproj': 8.0,
     'L0_attn_W_dt': 8.0,
     'L0_attn_b_dt': 8.0,
     'L0_attn_A_log': 8.0,
     'L0_attn_W_out': 8.0,
     'L0_ffn_router_w': 8.0,
     'L0_ffn_up_proj': 8.0,
     'L0_ffn_gate_proj': 8.0,
     'L0_ffn_down_proj': 8.0,
     'L0_ffn_sh_gate': 8.0,
     'L0_ffn_sh_up': 8.0,
     'L0_ffn_sh_down': 8.0}
    for name, (base, spread) in spreads.items():
        noise = np.random.default_rng([zlib.crc32(name.encode()), seed]).standard_normal(out[name].shape)
        drawn = base * np.exp(spread * noise) if base else spread * noise
        out[name] = jnp.asarray(drawn.astype(out[name].dtype))
    for name, factor in factors.items():
        out[name] = (out[name] * factor).astype(out[name].dtype)
    return out
```

```python
from contextlib import ExitStack

import concourse.bass as bass
from concourse import mybir

ALU = mybir.AluOpType
ACT = mybir.ActivationFunctionType
F32 = mybir.dt.float32
BF16 = mybir.dt.bfloat16
U32 = mybir.dt.uint32

P = 128
SEQS, T, D = 128, 64, 128
INNER = 2 * D
HALVES = INNER // P
STATES = 16
TAPS = 4
DT_RANK = 8
EXPERTS, EXPERT_DIM = 16, 64
CHUNK = 512
BLOCKS = CHUNK // P
CHUNKS = SEQS * T // CHUNK
CHUNK_SEQS = CHUNK // T
PAIRS = EXPERTS * EXPERT_DIM // P
PARTS = 3
LN_EPS = 1e-5


class Signal:

    def __init__(self, ctx, nc, name):
        self.name, self.sem, self.count = name, ctx.enter_context(nc.semaphore(name)), 0

    def raised(self, by):
        self.count += by
        return (self, self.count)


class Slot:

    def __init__(self, tensor):
        self.whole, self.readers, self.held = tensor, [], False

    def release(self, *tokens):
        self.readers, self.held = list(tokens), False


class Ring:

    def __init__(self, tensors):
        self.slots = [Slot(t) for t in tensors]

    def take(self, queue, blocks=False):
        slot = next(s for s in self.slots if not s.held)
        slot.t = slot.whole[:, :].rearrange("p (q n) -> p q n", q=BLOCKS) if blocks else slot.whole
        self.slots.remove(slot)
        self.slots.append(slot)
        queue.wait(*slot.readers)
        slot.held = True
        return slot


class Queue:

    def __init__(self):
        self.ops, self.passed = [], {}

    def wait(self, *tokens):
        for signal, value in tokens:
            if self.passed.get(signal.name, 0) < value:
                self.passed[signal.name] = value
                self.ops.append(lambda e, s=signal.sem, v=value: e.wait_ge(s, v))

    def put(self, op, signal, by=1):
        if signal is None:
            self.ops.append(op)
            return None
        self.ops.append(lambda e: op(e).then_inc(signal.sem, by))
        return signal.raised(by)

    def emit(self, engine):
        for op in self.ops:
            op(engine)

    def load(self, dst, src, signal):
        return self.put(lambda e: e.dma_start(dst, src), signal, 16)

    def matmul(self, out, lhsT, rhs, start=True, stop=True, signal=None):
        return self.put(lambda e: e.matmul(out, lhsT, rhs, start=start, stop=stop, skip_group_check=True), signal)

    def transpose(self, out, in_, identity, start=True, stop=True, signal=None):
        return self.put(lambda e: e.matmul(out, in_, identity, is_transpose=True, start=start, stop=stop,
                                           skip_group_check=True), signal)

    def act(self, out, in_, func, signal, bias=None, scale=1.0):
        if bias is None:
            return self.put(lambda e: e.activation(out, in_, func, scale=scale), signal)
        return self.put(lambda e: e.activation(out, in_, func, bias=bias, scale=scale), signal)

    def copy(self, out, in_, signal):
        return self.put(lambda e: e.tensor_copy(out, in_), signal)

    def fill(self, out, value, signal):
        return self.put(lambda e: e.memset(out, value), signal)

    def reciprocal(self, out, in_, signal):
        return self.put(lambda e: e.reciprocal(out, in_), signal)

    def bn_stats(self, out, in_, signal):
        return self.put(lambda e: e.bn_stats(out, in_), signal)

    def bn_aggr(self, out, in_, signal):
        return self.put(lambda e: e.bn_aggr(out, in_), signal)

    def max8(self, out, in_, signal):
        return self.put(lambda e: e.max(out, in_), signal)

    def max8_index(self, out, values, in_, signal):
        return self.put(lambda e: e.max_index(out, values, in_), signal)

    def scan(self, out, factor, addend, signal):
        return self.put(lambda e: e.tensor_tensor_scan(out, factor, addend, 0.0, ALU.mult, ALU.add), signal)

    def tt(self, out, a, b, op, signal):
        return self.put(lambda e: e.tensor_tensor(out, a, b, op), signal)

    def ts(self, out, a, s1, s2, op0, op1, signal):
        return self.put(lambda e: e.tensor_scalar(out, a, s1, s2, op0, op1), signal)

    def stt(self, out, a, scalar, b, op0, op1, signal):
        return self.put(lambda e: e.scalar_tensor_tensor(out=out, in0=a, scalar=scalar, in1=b, op0=op0, op1=op1),
                        signal)


def decoder_layer(nc, io, out_dram):
    ctx = ExitStack()
    with ctx:
        names = iter(range(10000))

        def sb(name, shape, dt=F32):
            return ctx.enter_context(nc.sbuf_tensor(name, shape, dt))

        def ring(name, n, shape, dt=F32):
            return Ring([sb(f"{name}{i}", shape, dt) for i in range(n)])

        def sig(name):
            return Signal(ctx, nc, "s_" + name)

        banks = Ring([ctx.enter_context(nc.psum_tensor(f"bank{i}", [P, CHUNK], F32)) for i in range(4)])
        b_bank = Ring([ctx.enter_context(nc.psum_tensor("b_bank", [P, CHUNK], F32))])
        down_bank = Ring([ctx.enter_context(nc.psum_tensor("down_bank", [P, BLOCKS, D], F32))])
        y_banks = Ring([ctx.enter_context(nc.psum_tensor("y_banks", [P, BLOCKS, INNER], F32))])

        pe, act, dve, pool, sync = Queue(), Queue(), Queue(), Queue(), Queue()

        ident = sb("ident", [P, P])
        ident16 = sb("ident16", [P, P], BF16)
        w_in = sb("w_in", [P, 2 * INNER])
        w_xproj = sb("w_xproj", [P, HALVES, DT_RANK + 2 * STATES])
        w_xproj_half = sb("w_xproj_half", [P, HALVES, DT_RANK + 2 * STATES])
        w_dt = sb("w_dt", [DT_RANK, INNER])
        w_out = sb("w_out", [P, HALVES, D])
        conv_w = sb("conv_w", [P, HALVES, TAPS])
        conv_b = sb("conv_b", [P, HALVES])
        b_dt = sb("b_dt", [P, HALVES])
        d_param = sb("d_param", [P, HALVES])
        a_log = sb("a_log", [P, HALVES, STATES])
        a_exp = sb("a_exp", [P, HALVES, STATES])
        a_neg = sb("a_neg", [P, HALVES, STATES])
        w_q, w_k, w_v = sb("w_q", [P, D]), sb("w_k", [P, D]), sb("w_v", [P, D])
        w_q_swap, w_k_swap = sb("w_q_swap", [P, D]), sb("w_k_swap", [P, D])
        xpos = sb("xpos", [P, 4, T])
        decay_mask = sb("decay_mask", [P, P])
        router_rows = sb("router_rows", [EXPERTS, D])
        w_router = sb("w_router", [P, EXPERTS])
        router_bias = sb("router_bias", [P, EXPERTS])
        expert_no = sb("expert_no", [P, EXPERTS])
        up_w = sb("up_w", [P, EXPERTS, EXPERT_DIM])
        gate_w = sb("gate_w", [P, EXPERTS, EXPERT_DIM])
        down_w = sb("down_w", [P, PAIRS, D])
        shared_rows = sb("shared_rows", [P, 3, P])
        shared_w = sb("shared_w", [P, 3, P])
        pick_bc_rows = sb("pick_bc_rows", [PARTS * 2 * STATES, 2 * STATES])
        pick_bc = sb("pick_bc", [PARTS * 2 * STATES, 2 * STATES, P], BF16)
        pick_expert_rows = sb("pick_expert_rows", [PARTS * EXPERTS, EXPERTS])
        pick_expert = sb("pick_expert", [PARTS * EXPERTS, EXPERTS, EXPERT_DIM], BF16)
        minus_half = sb("minus_half", [P, BLOCKS])

        x_ring = [sb(f"x{i}", [P, BLOCKS, D]) for i in range(4)]
        ctx_ring = [sb(f"ctx{i}", [P, BLOCKS, D]) for i in range(2)]
        xc2_r = ring("xc2", 1, [P, HALVES, CHUNK])
        z_tanh_r = ring("z_tanh", 2, [P, 2, INNER])
        gate_z_r = ring("gate_z", 2, [P, BLOCKS, INNER])
        skip_r = ring("skip", 2, [P, HALVES, CHUNK])
        bc_parts_r = ring("bc_parts", 1, [P, BLOCKS, PARTS, 2 * STATES], BF16)
        bc_rest_r = ring("bc_rest", 1, [P, BLOCKS, 2 * STATES])
        dt_low_r = ring("dt_low", 1, [P, BLOCKS, DT_RANK])
        dt_lowT_r = ring("dt_lowT", 1, [DT_RANK, CHUNK])
        bcT_r = ring("bcT", 2, [PARTS * 2 * STATES, CHUNK], BF16)
        delta_r = ring("delta", 2, [P, HALVES, CHUNK])
        dx_r = ring("dx", 2, [P, HALVES, CHUNK])

        narrow_r = ring("narrow", 18, [P, CHUNK])
        wide_r = ring("wide", 6, [P, HALVES, CHUNK])
        decay_r = ring("decay", 3, [P, HALVES, CHUNK])
        drive_r = ring("drive", 2, [P, HALVES, CHUNK])
        state_r = ring("state", 2, [P, HALVES, CHUNK])
        c_r = ring("c_all", 3, [P, CHUNK])
        read_r = ring("read", 3, [P, HALVES, CHUNK])

        x2_r = ring("x2", 2, [P, CHUNK])

        stats_r = ring("stats", 3, [P, BLOCKS, 6])
        moments_r = ring("moments", 3, [P, BLOCKS, 2])
        var_eps_r = ring("var_eps", 3, [P, BLOCKS])
        rstd_r = ring("rstd", 3, [P, BLOCKS])

        logits_r = ring("logits", 1, [P, BLOCKS, EXPERTS])
        top_r = ring("top", 1, [P, BLOCKS, 8])
        top_at_r = ring("top_at", 1, [P, BLOCKS, 8], U32)
        top_f_r = ring("top_f", 1, [P, BLOCKS, 2])
        soft_r = ring("soft", 1, [P, 4, BLOCKS])
        comb_r = ring("comb", 1, [P, 3, BLOCKS, EXPERTS])
        comb_parts_r = ring("comb_parts", 1, [P, BLOCKS, PARTS, EXPERTS], BF16)
        comb_rest_r = ring("comb_rest", 1, [P, BLOCKS, EXPERTS])
        combT_r = ring("combT", 1, [PARTS * EXPERTS, CHUNK], BF16)

        s = {n: sig(n) for n in (
            "consts", "setup_act", "setup_dve", "setup_pe", "setup_pool",
            "xT_mm", "xT", "xb_mm", "conv_bias", "conv_taps", "z_mm", "z_tanh", "gate_z", "conv_tanh", "xc2", "skip",
            "proj_mm", "dt_low", "bc_split", "bcT_mm", "bcT", "dt_lowT_mm", "dt_lowT", "dt_mm", "dt_pre",
            "dt_e", "dt_ln", "dt_dve", "delta", "dx",
            "decay", "c_mm", "c_all", "b_mm", "drive", "state", "read", "y_acc",
            "y_gated", "y_gatedT_mm", "y_gatedT", "out_mm", "sum", "stats", "moments", "var_eps", "rstd", "normed",
            "ctxT_mm", "ctxT", "x1T_mm", "x1T", "q_mm", "q_rot", "q", "k_mm", "k_rot", "k", "v_mm", "v", "score_mm", "ret",
            "retout_mm",
            "x2T_mm", "x2T", "router_mm", "router", "top_exp", "comb_split", "combT_mm", "combT", "comb_mm", "comb_all",
            "gu_mm", "g_tanh", "g_silu", "gu", "hid", "down_mm")}
        s_x = [sig(f"x_load{i}") for i in range(len(x_ring))]
        s_ctx = [sig(f"ctx_load{i}") for i in range(len(ctx_ring))]
        s_store = [sig(f"store{i}") for i in range(2)]

        x_view = io["x"].rearrange("b t d -> (b t) d").rearrange("(c q p) d -> c p q d", p=P, q=BLOCKS)
        ctx_view = io["ctx_1024"].rearrange("b t d -> (b t) d").rearrange("(c q p) d -> c p q d", p=P, q=BLOCKS)
        out_view = out_dram.rearrange("b t d -> (b t) d").rearrange("(c q p) d -> c p q d", p=P, q=BLOCKS)
        x_free = [[] for _ in x_ring]
        ctx_free = [[] for _ in ctx_ring]

        def load_x(c):
            i = c % len(x_ring)
            sync.wait(*x_free[i])
            return sync.load(x_ring[i][:, :, :], x_view[c], s_x[i])

        def load_ctx(c):
            i = c % len(ctx_ring)
            sync.wait(*ctx_free[i])
            return sync.load(ctx_ring[i][:, :, :], ctx_view[c], s_ctx[i])

        x_loaded, ctx_loaded = {}, {}

        def const(dst, src):
            return sync.load(dst, src, s["consts"])

        def per_channel(dst, vector):
            for h in range(HALVES):
                const(dst[:, h:h + 1], vector[h * P:(h + 1) * P].rearrange("(p a) -> p a", a=1))

        const(ident[:, :], io["c_ident"])
        x_loaded[0] = load_x(0)
        const(w_in[:, :], io["L0_attn_W_in"])
        const(conv_w[:, :, :], io["L0_attn_conv_w"].rearrange("(h p) k -> p h k", p=P))
        per_channel(conv_b, io["L0_attn_conv_b"])
        const(w_xproj[:, :, :], io["L0_attn_W_xproj"].rearrange("(h p) n -> p h n", p=P))
        const(w_dt[:, :], io["L0_attn_W_dt"])
        per_channel(b_dt, io["L0_attn_b_dt"])
        const(a_log[:, :, :], io["L0_attn_A_log"].rearrange("(h p) n -> p h n", p=P))
        per_channel(d_param, io["L0_attn_D_param"])
        const(pick_bc_rows[:, :], io["c_pick_bc"])
        early = const(pick_expert_rows[:, :], io["c_pick_expert"])
        const(w_out[:, :, :], io["L0_attn_W_out"].rearrange("(h p) n -> p h n", p=P))
        qkv_rows = [slot.whole for slot in narrow_r.slots[0:3]]
        for rows_at, name in zip(qkv_rows, ("Wq", "Wk", "Wv")):
            const(rows_at[:, 0:D], io["L0_xattn_" + name])
        const(xpos[:, :, :], io["c_xpos"])
        const(decay_mask[:, :], io["c_decay_mask"])
        const(router_rows[:, :], io["L0_ffn_router_w"])
        const(router_bias[:, :], io["L0_ffn_router_bias"].rearrange("(a n) -> a n", a=1).partition_broadcast(P))
        const(expert_no[:, :], io["c_expert_no"])
        const(shared_rows[:, 0, :], io["L0_ffn_sh_gate"])
        const(shared_rows[:, 1, :], io["L0_ffn_sh_up"])
        const(shared_rows[:, 2, :], io["L0_ffn_sh_down"])
        const(gate_w[:, :, :], io["L0_ffn_gate_proj"].rearrange("k d e -> d k e"))
        const(up_w[:, :, :], io["L0_ffn_up_proj"].rearrange("k d e -> d k e"))
        late = const(down_w[:, :, :], io["L0_ffn_down_proj"].rearrange("k e d -> (k e) d")
                     .rearrange("(j p) d -> p j d", p=P))
        del early
        weights_in = late

        for queue in (act, dve, pool, pe):
            queue.wait(weights_in)
        dve.copy(ident16[:, :], ident[:, :], s["setup_dve"])
        dve.ts(w_xproj_half[:, :, :], w_xproj[:, :, :], 0.5, 1.0, ALU.mult, ALU.mult, s["setup_dve"])
        dve.copy(pick_bc[:, :, :], pick_bc_rows[:, :].unsqueeze(2).to_broadcast([PARTS * 2 * STATES, 2 * STATES, P]),
                 s["setup_dve"])
        for slot in decay_r.slots:
            zero_decay = dve.fill(slot.whole[:, :, :].rearrange("p h (b t) -> p (h b) t", t=T)[:, :, 0:1], 0.0,
                                  s["setup_dve"])
        a_exp_done = act.act(a_exp[:, :, :], a_log[:, :, :], ACT.Exp, s["setup_act"])
        dve.wait(a_exp_done)
        setup_dve = dve.ts(a_neg[:, :, :], a_exp[:, :, :], -1.0, 1.0, ALU.mult, ALU.mult, s["setup_dve"])
        pool.copy(pick_expert[:, :, :],
                  pick_expert_rows[:, :].unsqueeze(2).to_broadcast([PARTS * EXPERTS, EXPERTS, EXPERT_DIM]),
                  s["setup_pool"])
        setup_pool = pool.fill(minus_half[:, :], -0.5, s["setup_pool"])
        bank = banks.take(pe)
        for i in range(3):
            pe.transpose(bank.t[:, i * P:(i + 1) * P], shared_rows[:, i, :], ident[:, :])
        flipped = pe.transpose(bank.t[:, 3 * P:3 * P + EXPERTS], router_rows[:, :], ident[0:EXPERTS, 0:EXPERTS],
                               signal=s["setup_pe"])
        act.wait(flipped)
        act.act(shared_w[:, :, :], bank.t[:, 0:3 * P].rearrange("p (i n) -> p i n", i=3), ACT.Copy, s["setup_act"])
        setup_act = act.act(w_router[:, :], bank.t[:, 3 * P:3 * P + EXPERTS], ACT.Copy, s["setup_act"])
        bank.release(setup_act)
        bank = banks.take(pe)
        for i in range(3):
            flipped = pe.transpose(bank.t[:, i * P:(i + 1) * P], qkv_rows[i][:, 0:D], ident[:, :],
                                   signal=s["setup_pe"])
        act.wait(flipped)
        for i, w in enumerate((w_q, w_k, w_v)):
            qkv_done = act.act(w[:, :], bank.t[:, i * P:(i + 1) * P], ACT.Copy, s["setup_act"])
        bank.release(qkv_done)
        dve.wait(qkv_done)
        for w, swapped in ((w_q, w_q_swap), (w_k, w_k_swap)):
            from_pairs, to_pairs = (a[:, :].rearrange("p (n two) -> p n two", two=2) for a in (w, swapped))
            for i in (0, 1):
                setup_dve = dve.copy(to_pairs[:, :, i], from_pairs[:, :, 1 - i], s["setup_dve"])
        setup_act = qkv_done
        for queue in (pe, act, dve, pool):
            queue.wait(setup_dve, setup_act, setup_pool)

        def seqs(ap):
            return ap.rearrange("p (b t) -> p b t", t=T)

        prepared = {}

        def prepare(c):
            if c + 1 < CHUNKS:
                x_loaded[c + 1] = load_x(c + 1)
            x_tok = x_ring[c % len(x_ring)]
            bank = banks.take(pe)
            pe.wait(x_loaded[c])
            for q in range(BLOCKS):
                done = pe.transpose(bank.t[:, q * P:(q + 1) * P], x_tok[:, q, :], ident[:, :],
                                    signal=s["xT_mm"] if q == BLOCKS - 1 else None)
            xT = narrow_r.take(act)
            act.wait(done)
            xT_done = act.act(xT.t[:, :], bank.t[:, :], ACT.Copy, s["xT"])
            bank.release(xT_done)
            yield
            conv = wide_r.take(act)
            for h in range(HALVES):
                bank = banks.take(pe)
                pe.wait(xT_done)
                done = pe.matmul(bank.t[:, :], w_in[:, h * P:(h + 1) * P], xT.t[:, :], signal=s["xb_mm"])
                act.wait(done)
                tap = act.act(conv.t[:, h, :], bank.t[:, :], ACT.Identity, s["conv_bias"],
                              bias=conv_b[:, h:h + 1], scale=conv_w[:, h, TAPS - 1:TAPS])
                for k in range(1, TAPS):
                    dve.wait(tap)
                    late_out = seqs(conv.t[:, h, :])[:, :, k:T]
                    tap = dve.stt(late_out, seqs(bank.t[:, :])[:, :, 0:T - k], conv_w[:, h, TAPS - 1 - k:TAPS - k],
                                  late_out, ALU.mult, ALU.add, s["conv_taps"])
                bank.release(tap)
                yield
            gate_z = gate_z_r.take(dve)
            for g in range(2):
                bank = banks.take(pe)
                for q in (0, 1):
                    block = 2 * g + q
                    z_done = pe.matmul(bank.t[:, q * INNER:(q + 1) * INNER], xT.t[:, block * P:(block + 1) * P],
                                       w_in[:, INNER:2 * INNER], signal=s["z_mm"] if q else None)
                z_tanh = z_tanh_r.take(act)
                act.wait(z_done)
                done = act.act(z_tanh.t[:, :, :], bank.t[:, :].rearrange("p (q n) -> p q n", q=2), ACT.Tanh,
                               s["z_tanh"], scale=0.5)
                dve.wait(done)
                gate_done = dve.stt(gate_z.t[:, 2 * g:2 * g + 2, :], z_tanh.t[:, :, :], 1.0,
                                    bank.t[:, :].rearrange("p (q n) -> p q n", q=2), ALU.add, ALU.mult, s["gate_z"])
                bank.release(gate_done)
                z_tanh.release(gate_done)
                yield
            xT.release(z_done)
            conv_tanh = wide_r.take(act)
            act.wait(tap)
            done = act.act(conv_tanh.t[:, :, :], conv.t[:, :, :], ACT.Tanh, s["conv_tanh"], scale=0.5)
            xc2 = xc2_r.take(dve)
            dve.wait(done)
            xc2_done = dve.stt(xc2.t[:, :, :], conv_tanh.t[:, :, :], 1.0, conv.t[:, :, :], ALU.add, ALU.mult, s["xc2"])
            conv.release(xc2_done)
            conv_tanh.release(xc2_done)
            yield
            bank = banks.take(pe)
            pe.wait(xc2_done)
            proj = bank.t[:, 0:BLOCKS * (DT_RANK + 2 * STATES)].rearrange("p (q n) -> p q n", q=BLOCKS)
            for q in range(BLOCKS):
                for h in range(HALVES):
                    done = pe.matmul(proj[:, q, :], xc2.t[:, h, q * P:(q + 1) * P], w_xproj_half[:, h, :],
                                     start=h == 0, stop=h == HALVES - 1,
                                     signal=s["proj_mm"] if (q, h) == (BLOCKS - 1, HALVES - 1) else None)
            proj_done = done
            skip = skip_r.take(dve)
            dve.wait(xc2_done)
            for h in range(HALVES):
                skip_done = dve.ts(skip.t[:, h, :], xc2.t[:, h, :], d_param[:, h:h + 1], 0.5, ALU.mult, ALU.mult,
                                   s["skip"])
            yield
            parts, rest = bc_parts_r.take(dve), bc_rest_r.take(dve)
            bc = proj[:, :, DT_RANK:]
            dve.wait(proj_done)
            done = dve.copy(parts.t[:, :, 0, :], bc, s["bc_split"])
            dve.wait(done)
            rest_done = dve.tt(rest.t[:, :, :], bc, parts.t[:, :, 0, :], ALU.subtract, s["bc_split"])
            dt_low = dt_low_r.take(act)
            act.wait(rest_done)
            low_done = act.act(dt_low.t[:, :, :], proj[:, :, 0:DT_RANK], ACT.Copy, s["dt_low"])
            bank.release(low_done)
            dve.wait(rest_done)
            done = dve.copy(parts.t[:, :, 1, :], rest.t[:, :, :], s["bc_split"])
            dve.wait(done)
            split_done = dve.tt(parts.t[:, :, 2, :], rest.t[:, :, :], parts.t[:, :, 1, :], ALU.subtract, s["bc_split"])
            rest.release(split_done)
            yield
            bank = banks.take(pe)
            pe.wait(low_done)
            for q in range(BLOCKS):
                done = pe.transpose(bank.t[0:DT_RANK, q * P:(q + 1) * P], dt_low.t[:, q, :], ident[:, :],
                                    signal=s["dt_lowT_mm"] if q == BLOCKS - 1 else None)
            dt_low.release(done)
            dt_lowT = dt_lowT_r.take(act)
            act.wait(done)
            lowT_done = act.act(dt_lowT.t[:, :], bank.t[0:DT_RANK, :], ACT.Copy, s["dt_lowT"])
            bank.release(lowT_done)
            bank = banks.take(pe)
            rows = PARTS * 2 * STATES
            bcT_bank = bank.t[:, :].bitcast(BF16)[0:rows, 0:CHUNK]
            pe.wait(split_done)
            for q in range(BLOCKS):
                done = pe.transpose(bcT_bank[:, q * P:(q + 1) * P],
                                    parts.t[:, q, :, :].rearrange("p a n -> p (a n)"), ident16[:, :],
                                    signal=s["bcT_mm"] if q == BLOCKS - 1 else None)
            parts.release(done)
            bcT = bcT_r.take(act)
            act.wait(done)
            bcT_done = act.act(bcT.t[:, :], bcT_bank, ACT.Copy, s["bcT"])
            bank.release(bcT_done)
            yield
            dt_abs, dt_relu = wide_r.take(act), wide_r.take(act)
            for h in range(HALVES):
                bank = banks.take(pe)
                pe.wait(lowT_done)
                dt_done = pe.matmul(bank.t[:, :], w_dt[:, h * P:(h + 1) * P], dt_lowT.t[:, :], signal=s["dt_mm"])
                act.wait(dt_done)
                act.act(dt_abs.t[:, h, :], bank.t[:, :], ACT.Abs, s["dt_pre"], bias=b_dt[:, h:h + 1])
                pre_done = act.act(dt_relu.t[:, h, :], bank.t[:, :], ACT.Relu, s["dt_pre"], bias=b_dt[:, h:h + 1])
                bank.release(pre_done)
            dt_lowT.release(dt_done)
            yield
            dt_e, dt_ln = wide_r.take(act), wide_r.take(act)
            act.wait(pre_done)
            e_done = act.act(dt_e.t[:, :, :], dt_abs.t[:, :, :], ACT.Exp, s["dt_e"], scale=-1.0)
            dt_abs.release(e_done)
            act.wait(e_done)
            ln_done = act.act(dt_ln.t[:, :, :], dt_e.t[:, :, :], ACT.Ln, s["dt_ln"], bias=1.0)
            dt_w = wide_r.take(dve)
            dve.wait(e_done)
            done = dve.ts(dt_w.t[:, :, :], dt_e.t[:, :, :], 1.0, -1.0, ALU.add, ALU.add, s["dt_dve"])
            dve.wait(done)
            residue = dve.stt(dt_w.t[:, :, :], dt_w.t[:, :, :], -1.0, dt_e.t[:, :, :], ALU.mult, ALU.add, s["dt_dve"])
            dt_e.release(ln_done, residue)
            yield
            pool.wait(residue, ln_done)
            log1p = pool.tt(dt_ln.t[:, :, :], dt_ln.t[:, :, :], dt_w.t[:, :, :], ALU.add, s["delta"])
            dt_w.release(log1p)
            delta = delta_r.take(pool)
            pool.wait(log1p)
            delta_done = pool.tt(delta.t[:, :, :], dt_ln.t[:, :, :], dt_relu.t[:, :, :], ALU.add, s["delta"])
            dt_ln.release(delta_done)
            dt_relu.release(delta_done)
            yield
            dx = dx_r.take(dve)
            dve.wait(delta_done)
            dx_done = dve.stt(dx.t[:, :, :], xc2.t[:, :, :], 0.5, delta.t[:, :, :], ALU.mult, ALU.mult, s["dx"])
            xc2.release(dx_done, proj_done)
            prepared[c] = dict(delta=delta, dx=dx, skip=skip, bcT=bcT, gate_z=gate_z, delta_done=delta_done,
                               dx_done=dx_done, skip_done=skip_done, bcT_done=bcT_done, gate_done=gate_done)
            yield

        STEPS = CHUNKS * STATES
        decays, c_alls, b_alls, drives, states, reads, scanned = {}, {}, {}, {}, {}, {}, {}

        def make_decay(k):
            c, n = divmod(k, STATES)
            p = prepared[c]
            decay = decay_r.take(act)
            act.wait(p["delta_done"])
            for h in range(HALVES):
                done = act.act(seqs(decay.t[:, h, :])[:, :, 1:T], seqs(p["delta"].t[:, h, :])[:, :, 1:T], ACT.Exp,
                               s["decay"], scale=a_neg[:, h, n:n + 1])
            decays[k] = (decay, done)
            if n == STATES - 1:
                p["delta"].release(done, p["dx_done"])

        def spread_c(k):
            c, n = divmod(k, STATES)
            p = prepared[c]
            bank = banks.take(pe)
            pe.wait(p["bcT_done"])
            done = pe.matmul(bank.t[:, :], pick_bc[:, STATES + n, :], p["bcT"].t[:, :], signal=s["c_mm"])
            c_all = c_r.take(act)
            act.wait(done)
            copied = act.act(c_all.t[:, :], bank.t[:, :], ACT.Copy, s["c_all"])
            bank.release(copied)
            c_alls[k] = (c_all, copied)

        def spread_b(k):
            c, n = divmod(k, STATES)
            p = prepared[c]
            bank = b_bank.take(pe)
            pe.wait(p["bcT_done"])
            done = pe.matmul(bank.t[:, :], pick_bc[:, n, :], p["bcT"].t[:, :], signal=s["b_mm"])
            b_alls[k] = (bank, done)
            if n == STATES - 1:
                p["bcT"].release(done)

        def make_drive(k):
            c, n = divmod(k, STATES)
            p = prepared[c]
            bank, spread = b_alls.pop(k)
            drive = drive_r.take(dve)
            dve.wait(p["dx_done"], spread)
            done = dve.tt(drive.t[:, :, :], p["dx"].t[:, :, :],
                          bank.t[:, :].unsqueeze(1).to_broadcast([P, HALVES, CHUNK]), ALU.mult, s["drive"])
            bank.release(done)
            drives[k] = (drive, done)
            if n == STATES - 1:
                p["dx"].release(done)

        def scan(k):
            decay, decay_done = decays.pop(k)
            drive, drive_done = drives.pop(k)
            state = state_r.take(dve)
            dve.wait(decay_done, drive_done)
            flat = "p h n -> p (h n)"
            out, a, b = (x.t[:, :, :].rearrange(flat) for x in (state, decay, drive))
            done = dve.scan(out, a, b, s["state"])
            decay.release(done)
            drive.release(done)
            states[k] = (state, done)

        def read_state(k):
            state, scan_done = states.pop(k)
            c_all, copied = c_alls.pop(k)
            read = read_r.take(pool)
            pool.wait(scan_done, copied)
            done = pool.tt(read.t[:, :, :], state.t[:, :, :],
                           c_all.t[:, :].unsqueeze(1).to_broadcast([P, HALVES, CHUNK]), ALU.mult, s["read"])
            state.release(done)
            c_all.release(done)
            reads[k] = (read, done)

        def sum_states(k):
            c, n = divmod(k, STATES)
            p = prepared[c]
            if n == 0:
                p["y"] = y_banks.take(pe)
            y = p["y"].t
            read, read_done = reads.pop(k)
            pe.wait(read_done)
            for q in range(BLOCKS):
                for h in range(HALVES):
                    done = pe.transpose(y[:, q, h * P:(h + 1) * P], read.t[:, h, q * P:(q + 1) * P], ident[:, :],
                                        start=(n == 0 and h == 0 and q % 2 == 0), stop=False,
                                        signal=s["y_acc"] if (q, h) == (BLOCKS - 1, HALVES - 1) else None)
            read.release(done)
            if n == STATES - 1:
                pe.wait(p["skip_done"])
                for q in range(BLOCKS):
                    for h in range(HALVES):
                        done = pe.transpose(y[:, q, h * P:(h + 1) * P], p["skip"].t[:, h, q * P:(q + 1) * P],
                                            ident[:, :], start=False, stop=True,
                                            signal=s["y_acc"] if (q, h) == (BLOCKS - 1, HALVES - 1) else None)
                p["skip"].release(done)
                scanned[c] = done

        def scan_step(k):
            if k == 0:
                spread_b(0)
                for i in (0, 1):
                    make_decay(i)
                    spread_c(i)
                make_drive(0)
                spread_b(1)
            if k + 2 < STEPS:
                make_decay(k + 2)
                spread_c(k + 2)
            if k + 1 < STEPS:
                make_drive(k + 1)
            if k + 2 < STEPS:
                spread_b(k + 2)
            if k < STEPS:
                scan(k)
                read_state(k)
            if 2 <= k < STEPS + 2:
                sum_states(k - 2)

        def normalise(total, total_done, out_ring, queue_free=()):
            stats, moments, var_eps, rstd = (r.take(q) for r, q in (
                (stats_r, dve), (moments_r, dve), (var_eps_r, pool), (rstd_r, pool)))
            dve.wait(total_done)
            for q in range(BLOCKS):
                done = dve.bn_stats(stats.t[:, q, :], total.t[:, q, :], s["stats"])
            dve.wait(done)
            for q in range(BLOCKS):
                done = dve.bn_aggr(moments.t[:, q, :], stats.t[:, q, :], s["moments"])
            stats.release(done)
            pool.wait(done)
            eps_done = pool.ts(var_eps.t[:, :], moments.t[:, :, 1], LN_EPS, 1.0, ALU.add, ALU.mult, s["var_eps"])
            pool.wait(eps_done)
            rstd_done = pool.tt(rstd.t[:, :], var_eps.t[:, :], minus_half[:, :], ALU.pow, s["rstd"])
            var_eps.release(rstd_done)
            yield
            out = out_ring.take(dve, blocks=True)
            dve.wait(rstd_done)
            for q in range(BLOCKS):
                done = dve.ts(out.t[:, q, :], total.t[:, q, :], moments.t[:, q, 0:1], rstd.t[:, q:q + 1],
                              ALU.subtract, ALU.mult, s["normed"])
            total.release(done)
            moments.release(done)
            rstd.release(done)
            yield out, done

        def to_channels(src, src_done, ring_out, mm_signal, signal):
            bank = banks.take(pe)
            pe.wait(src_done)
            for q in range(BLOCKS):
                done = pe.transpose(bank.t[:, q * P:(q + 1) * P], src[:, q, :], ident[:, :],
                                    signal=mm_signal if q == BLOCKS - 1 else None)
            out = ring_out.take(act)
            act.wait(done)
            copied = act.act(out.t[:, :], bank.t[:, :], ACT.Copy, signal)
            bank.release(copied)
            return out, done, copied

        def rotate(w, w_swap, src, src_done, table, out_ring, name):
            turned = []
            for i, weights in enumerate((w, w_swap)):
                bank = banks.take(pe)
                pe.wait(src_done)
                mm_done = pe.matmul(bank.t[:, :], weights[:, :], src[:, :], signal=s[name + "_mm"])
                rot = narrow_r.take(dve)
                dve.wait(mm_done)
                done = dve.tt(seqs(rot.t[:, :]), seqs(bank.t[:, :]),
                              xpos[:, 2 * table + i, :].unsqueeze(1).to_broadcast([P, CHUNK_SEQS, T]), ALU.mult,
                              s[name + "_rot"])
                bank.release(done)
                turned.append(rot)
            out = out_ring.take(pool)
            pool.wait(done)
            added = pool.tt(out.t[:, :], turned[0].t[:, :], turned[1].t[:, :], ALU.add, s[name])
            for rot in turned:
                rot.release(added)
            return out, added, mm_done

        attended = {}

        def attend(c):
            p = prepared[c]
            if c == 0:
                ctx_loaded[0] = load_ctx(0)
            if c + 1 < CHUNKS:
                ctx_loaded[c + 1] = load_ctx(c + 1)
            y_gated = wide_r.take(dve)
            gated_y = y_gated.t[:, :, :].rearrange("p h n -> p (h n)").rearrange("p (q n) -> p q n", q=BLOCKS)
            dve.wait(scanned[c], p["gate_done"])
            for g in range(2):
                blocks = slice(2 * g, 2 * g + 2)
                gated = dve.stt(gated_y[:, blocks, :], p["gate_z"].t[:, blocks, :], 0.5, p["y"].t[:, blocks, :],
                                ALU.mult, ALU.mult, s["y_gated"])
            p["y"].release(gated)
            p["gate_z"].release(gated)
            yield
            y_gatedT = wide_r.take(act)
            for h in range(HALVES):
                bank = banks.take(pe)
                pe.wait(gated)
                for q in range(BLOCKS):
                    flipped = pe.transpose(bank.t[:, q * P:(q + 1) * P], gated_y[:, q, h * P:(h + 1) * P],
                                           ident[:, :], signal=s["y_gatedT_mm"] if q == BLOCKS - 1 else None)
                act.wait(flipped)
                copied = act.act(y_gatedT.t[:, h, :], bank.t[:, :], ACT.Copy, s["y_gatedT"])
                bank.release(copied)
            y_gated.release(flipped)
            yield
            ctx_i = c % len(ctx_ring)
            ctxT, ctx_mm, ctxT_done = to_channels(ctx_ring[ctx_i], ctx_loaded[c], narrow_r, s["ctxT_mm"], s["ctxT"])
            ctx_free[ctx_i] = [ctx_mm]
            yield
            bank = banks.take(pe)
            pe.wait(copied)
            for q in range(BLOCKS):
                for h in range(HALVES):
                    mm = pe.matmul(bank.t[:, q * P:(q + 1) * P], y_gatedT.t[:, h, q * P:(q + 1) * P], w_out[:, h, :],
                                   start=h == 0, stop=h == HALVES - 1,
                                   signal=s["out_mm"] if (q, h) == (BLOCKS - 1, HALVES - 1) else None)
            y_gatedT.release(mm)
            total = narrow_r.take(dve, blocks=True)
            dve.wait(mm)
            x_i = c % len(x_ring)
            done = dve.tt(total.t[:, :, :], bank.t[:, :].rearrange("p (q n) -> p q n", q=BLOCKS),
                          x_ring[x_i][:, :, :], ALU.add, s["sum"])
            bank.release(done)
            x_free[x_i] = [done]
            yield
            k_t, k_done, mm = rotate(w_k, w_k_swap, ctxT.t, ctxT_done, 1, narrow_r, "k")
            yield
            norm = normalise(total, done, narrow_r)
            next(norm)
            yield
            bank = banks.take(pe)
            for q in range(BLOCKS):
                mm = pe.matmul(bank.t[:, q * P:(q + 1) * P], ctxT.t[:, q * P:(q + 1) * P], w_v[:, :],
                               signal=s["v_mm"] if q == BLOCKS - 1 else None)
            ctxT.release(mm)
            v = narrow_r.take(act, blocks=True)
            act.wait(mm)
            v_done = act.act(v.t[:, :, :], bank.t[:, :].rearrange("p (q n) -> p q n", q=BLOCKS), ACT.Copy, s["v"])
            bank.release(v_done)
            yield
            x1, x1_done = next(norm)
            yield
            x1T, x1T_mm, x1T_done = to_channels(x1.t, x1_done, narrow_r, s["x1T_mm"], s["x1T"])
            yield
            q_t, q_done, mm = rotate(w_q, w_q_swap, x1T.t, x1T_done, 0, narrow_r, "q")
            x1T.release(mm)
            yield
            bank = banks.take(pe)
            pe.wait(q_done, k_done)
            for q in range(BLOCKS):
                cols = slice(q * P, (q + 1) * P)
                mm = pe.matmul(bank.t[:, cols], k_t.t[:, cols], q_t.t[:, cols],
                               signal=s["score_mm"] if q == BLOCKS - 1 else None)
            k_t.release(mm)
            q_t.release(mm)
            ret = narrow_r.take(dve, blocks=True)
            dve.wait(mm)
            ret_done = dve.tt(ret.t[:, :, :], bank.t[:, :].rearrange("p (q n) -> p q n", q=BLOCKS),
                              decay_mask[:, :].unsqueeze(1).to_broadcast([P, BLOCKS, P]), ALU.mult, s["ret"])
            bank.release(ret_done)
            yield
            bank = banks.take(pe)
            pe.wait(ret_done, v_done)
            for q in range(BLOCKS):
                mm = pe.matmul(bank.t[:, q * P:(q + 1) * P], ret.t[:, q, :], v.t[:, q, :],
                               signal=s["retout_mm"] if q == BLOCKS - 1 else None)
            ret.release(mm)
            v.release(mm)
            total = narrow_r.take(dve, blocks=True)
            dve.wait(mm)
            done = dve.tt(total.t[:, :, :], bank.t[:, :].rearrange("p (q n) -> p q n", q=BLOCKS), x1.t[:, :, :],
                          ALU.add, s["sum"])
            bank.release(done)
            x1.release(done, x1T_mm)
            yield
            norm = normalise(total, done, x2_r)
            next(norm)
            yield
            attended[c] = next(norm)
            yield

        stored = {}

        def experts(c):
            x2, x2_done = attended[c]
            x2T, x2T_mm, x2T_done = to_channels(x2.t, x2_done, narrow_r, s["x2T_mm"], s["x2T"])
            yield
            bank = banks.take(pe)
            pe.wait(x2T_done)
            scores = bank.t[:, 0:BLOCKS * EXPERTS].rearrange("p (q n) -> p q n", q=BLOCKS)
            for q in range(BLOCKS):
                mm = pe.matmul(scores[:, q, :], x2T.t[:, q * P:(q + 1) * P], w_router[:, :],
                               signal=s["router_mm"] if q == BLOCKS - 1 else None)
            logits = logits_r.take(dve)
            dve.wait(mm)
            done = dve.tt(logits.t[:, :, :], scores, router_bias[:, :].unsqueeze(1).to_broadcast([P, BLOCKS, EXPERTS]),
                          ALU.add, s["router"])
            bank.release(done)
            top, top_at = top_r.take(dve), top_at_r.take(dve)
            dve.wait(done)
            for q in range(BLOCKS):
                done = dve.max8(top.t[:, q, :], logits.t[:, q, :], s["router"])
            dve.wait(done)
            for q in range(BLOCKS):
                at_done = dve.max8_index(top_at.t[:, q, :], top.t[:, q, :], logits.t[:, q, :], s["router"])
            logits.release(at_done)
            yield
            soft = soft_r.take(dve)
            dve.wait(at_done)
            done = dve.tt(soft.t[:, 0, :], top.t[:, :, 1], top.t[:, :, 0], ALU.subtract, s["router"])
            top.release(done)
            act.wait(done)
            e_done = act.act(soft.t[:, 1, :], soft.t[:, 0, :], ACT.Exp, s["top_exp"])
            top_f = top_f_r.take(dve)
            f_done = dve.copy(top_f.t[:, :, :], top_at.t[:, :, 0:2], s["router"])
            top_at.release(f_done)
            yield
            dve.wait(e_done)
            done = dve.ts(soft.t[:, 0, :], soft.t[:, 1, :], 1.0, 1.0, ALU.add, ALU.mult, s["router"])
            dve.wait(done)
            done = dve.reciprocal(soft.t[:, 2, :], soft.t[:, 0, :], s["router"])
            dve.wait(done)
            done = dve.tt(soft.t[:, 3, :], soft.t[:, 1, :], soft.t[:, 2, :], ALU.mult, s["router"])
            comb = comb_r.take(dve)
            dve.wait(done, f_done)
            shape = [P, BLOCKS, EXPERTS]
            for i in (0, 1):
                eq = dve.tt(comb.t[:, i, :, :], expert_no[:, :].unsqueeze(1).to_broadcast(shape),
                            top_f.t[:, :, i].unsqueeze(2).to_broadcast(shape), ALU.is_equal, s["router"])
            dve.wait(eq)
            for i in (0, 1):
                done = dve.tt(comb.t[:, i, :, :], comb.t[:, i, :, :],
                              soft.t[:, 2 + i, :].unsqueeze(2).to_broadcast(shape), ALU.mult, s["router"])
            top_f.release(eq)
            soft.release(done)
            dve.wait(done)
            done = dve.tt(comb.t[:, 2, :, :], comb.t[:, 0, :, :], comb.t[:, 1, :, :], ALU.add, s["router"])
            parts, rest = comb_parts_r.take(dve), comb_rest_r.take(dve)
            whole = comb.t[:, 2, :, :]
            dve.wait(done)
            done = dve.copy(parts.t[:, :, 0, :], whole, s["comb_split"])
            dve.wait(done)
            done = dve.tt(rest.t[:, :, :], whole, parts.t[:, :, 0, :], ALU.subtract, s["comb_split"])
            comb.release(done)
            dve.wait(done)
            done = dve.copy(parts.t[:, :, 1, :], rest.t[:, :, :], s["comb_split"])
            dve.wait(done)
            split_done = dve.tt(parts.t[:, :, 2, :], rest.t[:, :, :], parts.t[:, :, 1, :], ALU.subtract,
                                s["comb_split"])
            rest.release(split_done)
            yield

            tiles = [None] + list(range(PAIRS))

            def up_and_gate(j):
                got = []
                for i, w in enumerate((gate_w, up_w)):
                    lhsT = shared_w[:, i, :] if j is None else w[:, 2 * j:2 * j + 2, :].rearrange("p k e -> p (k e)")
                    bank = banks.take(pe)
                    pe.wait(x2T_done)
                    got.append((bank, pe.matmul(bank.t[:, :], lhsT, x2T.t[:, :], signal=s["gu_mm"])))
                g_tanh = narrow_r.take(act)
                act.wait(got[0][1])
                tanh_done = act.act(g_tanh.t[:, :], got[0][0].t[:, :], ACT.Tanh, s["g_tanh"], scale=0.5)
                return got, g_tanh, tanh_done

            ahead = up_and_gate(tiles[0])
            yield
            bank = banks.take(pe)
            rows = PARTS * EXPERTS
            combT_bank = bank.t[:, :].bitcast(BF16)[0:rows, 0:CHUNK]
            pe.wait(split_done)
            for q in range(BLOCKS):
                mm = pe.transpose(combT_bank[:, q * P:(q + 1) * P],
                                  parts.t[:, q, :, :].rearrange("p a n -> p (a n)"), ident16[:, :],
                                  signal=s["combT_mm"] if q == BLOCKS - 1 else None)
            parts.release(mm)
            combT = combT_r.take(act)
            act.wait(mm)
            combT_done = act.act(combT.t[:, :], combT_bank, ACT.Copy, s["combT"])
            bank.release(combT_done)

            down = down_bank.take(pe)
            hidden = {}

            def down_project(i):
                hid, hid_done = hidden.pop(i)
                w = shared_w[:, 2, :] if tiles[i] is None else down_w[:, tiles[i], :]
                pe.wait(hid_done)
                for q in range(BLOCKS):
                    mm = pe.matmul(down.t[:, q, :], hid.t[:, q * P:(q + 1) * P], w, start=(i == 0 and q == 0),
                                   stop=i == len(tiles) - 1, signal=s["down_mm"] if q == BLOCKS - 1 else None)
                hid.release(mm)
                return mm

            for i, j in enumerate(tiles):
                got, g_tanh, tanh_done = ahead
                (g_bank, g_mm), (u_bank, u_mm) = got
                g_silu = narrow_r.take(dve)
                dve.wait(tanh_done, g_mm)
                silu_done = dve.stt(g_silu.t[:, :], g_tanh.t[:, :], 1.0, g_bank.t[:, :], ALU.add, ALU.mult,
                                    s["g_silu"])
                g_bank.release(silu_done)
                g_tanh.release(silu_done)
                target = (narrow_r if j is None else narrow_r).take(dve)
                dve.wait(silu_done, u_mm)
                gu_done = dve.stt(target.t[:, :], g_silu.t[:, :], 0.5, u_bank.t[:, :], ALU.mult, ALU.mult, s["gu"])
                u_bank.release(gu_done)
                g_silu.release(gu_done)
                if j is None:
                    hidden[i] = (target, gu_done)
                else:
                    bank = banks.take(pe)
                    pe.wait(combT_done)
                    mm = pe.matmul(bank.t[:, :], pick_expert[:, 2 * j:2 * j + 2, :].rearrange("p k e -> p (k e)"),
                                   combT.t[:, :], signal=s["comb_mm"])
                    comb_all = narrow_r.take(act)
                    act.wait(mm)
                    comb_done = act.act(comb_all.t[:, :], bank.t[:, :], ACT.Copy, s["comb_all"])
                    bank.release(comb_done)
                    hid = narrow_r.take(pool)
                    pool.wait(gu_done, comb_done)
                    hid_done = pool.tt(hid.t[:, :], target.t[:, :], comb_all.t[:, :], ALU.mult, s["hid"])
                    target.release(hid_done)
                    comb_all.release(hid_done)
                    hidden[i] = (hid, hid_done)
                if i + 1 < len(tiles):
                    ahead = up_and_gate(tiles[i + 1])
                if i >= 2:
                    down_project(i - 2)
                yield
            x2T.release(u_mm)
            combT.release(mm)
            down_project(len(tiles) - 2)
            yield
            mm = down_project(len(tiles) - 1)
            yield
            total = narrow_r.take(dve, blocks=True)
            dve.wait(mm)
            done = dve.tt(total.t[:, :, :], down.t[:, :, :], x2.t[:, :, :], ALU.add, s["sum"])
            down.release(done)
            x2.release(done, x2T_mm)
            norm = normalise(total, done, narrow_r)
            next(norm)
            yield
            y, y_done = next(norm)
            sync.wait(y_done)
            store = sync.load(out_view[c], y.t[:, :, :], s_store[c % 2])
            y.release(store)
            stored[c % 2] = store
            yield

        def tasks():
            for c in range(CHUNKS):
                if c:
                    yield prepare(c), STATES * (c - 1), STATES * (c - 1) + 13, 12
                yield attend(c), STATES * (c + 1) + 1, STATES * (c + 2) + 1, 15
                yield experts(c), STATES * (c + 2) + 1, STATES * (c + 3) + 1, 17

        for _ in prepare(0):
            pass
        plan = [dict(gen=g, first=a, last=b, n=n, done=0, over=False) for g, a, b, n in tasks()]
        for k in range(STATES * (CHUNKS + 3) + 2):
            scan_step(k)
            live = [t for t in plan if t["first"] <= k < t["last"] and not t["over"]]
            for t in live:
                t["goal"] = max(1, t["n"] * (k + 1 - t["first"]) / (t["last"] - t["first"]))
                if k == t["last"] - 1:
                    t["goal"] = 10000
            moved = True
            while moved:
                moved = False
                for t in live:
                    if t["done"] + 1 <= t["goal"] + 1e-9 and not t["over"]:
                        t["over"] = next(t["gen"], "end") == "end"
                        t["done"] += 1
                        moved = True
        assert all(t["over"] for t in plan)
        sync.wait(*stored.values())

        block = ctx.enter_context(nc.Block())

        @block.sync
        def _(eng):
            sync.emit(eng)

        @block.tensor
        def _(eng):
            pe.emit(eng)

        @block.scalar
        def _(eng):
            act.emit(eng)

        @block.vector
        def _(eng):
            dve.emit(eng)

        @block.gpsimd
        def _(eng):
            pool.emit(eng)


def shape_constants(np):
    f = np.float32
    pos = np.arange(T, dtype=np.float64)
    base = (np.arange(0, D, 2, dtype=np.float64) + 0.4 * D) / (1.4 * D)
    freqs = 1.0 / 10000.0 ** (np.arange(D // 2, dtype=np.float64) / (D // 2))
    scale = base[:, None] ** (pos[None, :] / 512.0)
    angle = freqs[:, None] * pos[None, :]
    sign = np.where(np.arange(D) % 2 == 0, -1.0, 1.0)[:, None]
    tables = []
    for factor in (scale, 1.0 / scale):
        tables += [np.repeat(np.cos(angle) * factor, 2, axis=0), np.repeat(np.sin(angle) * factor, 2, axis=0) * sign]
    key, query = np.arange(P)[:, None], np.arange(P)[None, :]
    mask = np.where((key // T == query // T) & (query >= key), 0.96875 ** np.maximum(query - key, 0.0), 0.0)

    def picks(n):
        return (np.arange(PARTS * n)[:, None] % n == np.arange(n)[None, :]).astype(f)

    return {
        "c_ident": np.eye(P, dtype=f),
        "c_xpos": np.ascontiguousarray(np.stack(tables, axis=1)).astype(f),
        "c_decay_mask": mask.astype(f),
        "c_pick_bc": picks(2 * STATES),
        "c_pick_expert": picks(EXPERTS),
        "c_expert_no": np.tile(np.arange(EXPERTS, dtype=f), (P, 1)),
    }


def kernel(**inputs):
    import numpy as _np
    import concourse.bacc as _bacc
    from concourse import mybir as _mybir
    from concourse.bass_utils import run_bass_kernel_spmd as _run

    nc = _bacc.Bacc("TRN2", target_bir_lowering=False, num_devices=1)
    arrays, io = {}, {}
    given = {n: _np.ascontiguousarray(a) for n, a in inputs.items()}
    for name, a in list(given.items()) + list(shape_constants(_np).items()):
        arrays[f"in_{name}_dram"] = a
        io[name] = nc.dram_tensor(f"in_{name}_dram", a.shape, _mybir.dt.from_np(a.dtype), kind="ExternalInput").ap()
    out = nc.dram_tensor("out_0_dram", (SEQS, T, D), F32, kind="ExternalOutput").ap()
    decoder_layer(nc, io, out)
    r = _run(nc, [arrays], core_ids=[0])
    return r.results[0]["out_0_dram"]
```

```python
from contextlib import ExitStack

import concourse.bass as bass
from concourse import mybir

ALU = mybir.AluOpType
ACT = mybir.ActivationFunctionType
F32 = mybir.dt.float32
BF16 = mybir.dt.bfloat16
U32 = mybir.dt.uint32

P = 128
SEQS, T, D = 128, 64, 128
INNER = 2 * D
HALVES = INNER // P
STATES = 16
TAPS = 4
DT_RANK = 8
EXPERTS, EXPERT_DIM = 16, 64
CHUNK = 512
BLOCKS = CHUNK // P
CHUNKS = SEQS * T // CHUNK
CHUNK_SEQS = CHUNK // T
PAIRS = EXPERTS * EXPERT_DIM // P
PARTS = 3
LN_EPS = 1e-5

class Signal:

    def __init__(self, ctx, nc, name):
        self.name, self.sem, self.count, self.times = name, ctx.enter_context(nc.semaphore(name)), 0, {}

    def raised(self, by, time):
        self.count += by
        self.times[self.count] = time
        return (self, self.count)


def time_of(tokens):
    return max([signal.times[value] for signal, value in tokens], default=0.0)


class Slot:

    def __init__(self, ring, tensor):
        self.ring, self.whole, self.readers = ring, tensor, []

    def release(self, *tokens):
        self.readers = list(tokens)
        self.ring.free.append(self)


class Ring:

    def __init__(self, tensors):
        self.free = [Slot(self, t) for t in tensors]

    def take(self, queue, blocks=False):
        slot = self.free.pop(0)
        slot.t = slot.whole[:, :].rearrange("p (q n) -> p q n", q=BLOCKS) if blocks else slot.whole
        queue.wait(*slot.readers)
        return slot


class Queue:

    def __init__(self, first=0.0, each=0.0, pointer=0.0, sends=0.0, sees=0.0):
        self.ops, self.passed, self.clock = [], {}, 0.0
        self.first, self.each, self.pointer, self.sends, self.sees = first, each, pointer, sends, sees

    def wait(self, *tokens):
        for signal, value in tokens:
            self.clock = max(self.clock, signal.times[value] + self.sees)
            if self.passed.get(signal.name, 0) < value:
                self.passed[signal.name] = value
                self.ops.append(lambda e, s=signal.sem, v=value: e.wait_ge(s, v))

    def put(self, op, signal, out=None, by=1, length=None):
        if length is None:
            length = self.first + self.each * out.free_size()
        self.clock += length
        if signal is None:
            self.ops.append(op)
            return None
        self.ops.append(lambda e: op(e).then_inc(signal.sem, by))
        return signal.raised(by, self.clock + self.sends)

    def emit(self, engine):
        for op in self.ops:
            op(engine)

    def load(self, dst, src, signal):
        return self.put(lambda e: e.dma_start(dst, src), signal, by=16, length=60.0)

    def matmul(self, out, lhsT, rhs, start=True, stop=True, signal=None):
        passes = 4 if rhs.dtype == F32 else 1
        return self.put(lambda e: e.matmul(out, lhsT, rhs, start=start, stop=stop, skip_group_check=True), signal,
                        length=max(out.free_size(), 64) * passes * 0.42)

    def transpose(self, out, in_, identity, start=True, stop=True, signal=None):
        return self.put(lambda e: e.matmul(out, in_, identity, is_transpose=True, start=start, stop=stop,
                                           skip_group_check=True), signal, length=115.0)

    def act(self, out, in_, func, signal, bias=None, scale=1.0):
        pointers = sum(not isinstance(x, float) for x in (0.0 if bias is None else bias, scale))
        length = self.first + self.each * out.free_size() + self.pointer * pointers
        if bias is None:
            return self.put(lambda e: e.activation(out, in_, func, scale=scale), signal, length=length)
        return self.put(lambda e: e.activation(out, in_, func, bias=bias, scale=scale), signal, length=length)

    def copy(self, out, in_, signal):
        return self.put(lambda e: e.tensor_copy(out, in_), signal, out)

    def fill(self, out, value, signal):
        return self.put(lambda e: e.memset(out, value), signal, out)

    def reciprocal(self, out, in_, signal):
        return self.put(lambda e: e.reciprocal(out, in_), signal, out)

    def bn_stats(self, out, in_, signal):
        return self.put(lambda e: e.bn_stats(out, in_), signal, in_)

    def bn_aggr(self, out, in_, signal):
        return self.put(lambda e: e.bn_aggr(out, in_), signal, in_)

    def max8(self, out, in_, signal):
        return self.put(lambda e: e.max(out, in_), signal, in_)

    def max8_index(self, out, values, in_, signal):
        return self.put(lambda e: e.max_index(out, values, in_), signal, in_, length=200.0)

    def scan(self, out, factor, addend, signal):
        return self.put(lambda e: e.tensor_tensor_scan(out, factor, addend, 0.0, ALU.mult, ALU.add), signal, out)

    def tt(self, out, a, b, op, signal):
        return self.put(lambda e: e.tensor_tensor(out, a, b, op), signal, out)

    def ts(self, out, a, s1, s2, op0, op1, signal):
        return self.put(lambda e: e.tensor_scalar(out, a, s1, s2, op0, op1), signal,
                        length=self.first + self.each * out.free_size() / 2
                        + self.pointer * sum(not isinstance(x, float) for x in (s1, s2)))

    def stt(self, out, a, scalar, b, op0, op1, signal):
        return self.put(lambda e: e.scalar_tensor_tensor(out=out, in0=a, scalar=scalar, in1=b, op0=op0, op1=op1),
                        signal, out)


def on(queue, *tokens, takes=()):
    return queue, tokens, takes


def start_time(need):
    queue, tokens, takes = need
    at = max(queue.clock, time_of(tokens) + queue.sees)
    for ring in set(takes):
        count = takes.count(ring)
        if len(ring.free) < count:
            return None
        for slot in ring.free[:count]:
            at = max(at, time_of(slot.readers) + queue.sees)
    return at


def run(streams):
    needs = {stream: next(stream) for stream in streams}
    while needs:
        for stream in [s for s in needs if needs[s][0] is None]:
            needs[stream] = next(stream, None)
        needs = {stream: need for stream, need in needs.items() if need is not None}
        starts = {stream: start_time(need) for stream, need in needs.items() if need[0] is not None}
        starts = {stream: at for stream, at in starts.items() if at is not None}
        if not needs:
            return
        assert starts, "no stream can go on"
        first = min(starts, key=starts.get)
        queue, latest = needs[first][0], starts[first] + MARGIN
        chosen = next(s for s in starts if needs[s][0] is queue and starts[s] <= latest)
        needs[chosen] = next(chosen, None)
        if needs[chosen] is None:
            del needs[chosen]


MARGIN = 1
NOT_YET = (None, (), ())


def decoder_layer(nc, io, out_dram):
    ctx = ExitStack()
    with ctx:
        names = iter(range(10000))

        def sb(name, shape, dt=F32):
            return ctx.enter_context(nc.sbuf_tensor(name, shape, dt))

        def ring(name, n, shape, dt=F32):
            return Ring([sb(f"{name}{i}", shape, dt) for i in range(n)])

        def sig(name):
            return Signal(ctx, nc, "s_" + name)

        banks = Ring([ctx.enter_context(nc.psum_tensor(f"bank{i}", [P, CHUNK], F32)) for i in range(4)])
        b_bank = Ring([ctx.enter_context(nc.psum_tensor("b_bank", [P, CHUNK], F32))])
        down_bank = Ring([ctx.enter_context(nc.psum_tensor("down_bank", [P, CHUNK], F32))])
        y_banks = Ring([ctx.enter_context(nc.psum_tensor("y_banks", [P, BLOCKS, INNER], F32))])

        pe, sync = Queue(sends=200.0, sees=85.0), Queue(sends=2000.0)
        act = Queue(70.0, 0.83, pointer=93.0, sends=100.0, sees=50.0)
        dve = Queue(70.0, 1.04, pointer=60.0, sends=80.0, sees=30.0)
        pool = Queue(150.0, 2.1, sends=30.0, sees=125.0)

        ident = sb("ident", [P, P])
        ident16 = sb("ident16", [P, P], BF16)
        w_in = sb("w_in", [P, 2 * INNER])
        w_xproj = sb("w_xproj", [P, HALVES, DT_RANK + 2 * STATES])
        w_xproj_half = sb("w_xproj_half", [P, HALVES, DT_RANK + 2 * STATES])
        w_dt = sb("w_dt", [DT_RANK, INNER])
        w_out = sb("w_out", [P, HALVES, D])
        conv_w = sb("conv_w", [P, HALVES, TAPS])
        conv_b = sb("conv_b", [P, HALVES])
        b_dt = sb("b_dt", [P, HALVES])
        d_param = sb("d_param", [P, HALVES])
        a_log = sb("a_log", [P, HALVES, STATES])
        a_exp = sb("a_exp", [P, HALVES, STATES])
        a_neg = sb("a_neg", [P, HALVES, STATES])
        w_q, w_k, w_v = sb("w_q", [P, D]), sb("w_k", [P, D]), sb("w_v", [P, D])
        w_q_swap, w_k_swap = sb("w_q_swap", [P, D]), sb("w_k_swap", [P, D])
        xpos = sb("xpos", [P, 4, T])
        decay_mask = sb("decay_mask", [P, P])
        router_rows = sb("router_rows", [EXPERTS, D])
        w_router = sb("w_router", [P, EXPERTS])
        router_bias = sb("router_bias", [P, EXPERTS])
        expert_no = sb("expert_no", [P, EXPERTS])
        up_w = sb("up_w", [P, EXPERTS, EXPERT_DIM])
        gate_w = sb("gate_w", [P, EXPERTS, EXPERT_DIM])
        down_w = sb("down_w", [P, PAIRS, D])
        shared_rows = sb("shared_rows", [P, 3, P])
        shared_w = sb("shared_w", [P, 3, P])
        pick_bc_rows = sb("pick_bc_rows", [PARTS * 2 * STATES, 2 * STATES])
        pick_bc = sb("pick_bc", [PARTS * 2 * STATES, 2 * STATES, P], BF16)
        pick_expert_rows = sb("pick_expert_rows", [PARTS * EXPERTS, EXPERTS])
        pick_expert = sb("pick_expert", [PARTS * EXPERTS, EXPERTS, EXPERT_DIM], BF16)
        minus_half = sb("minus_half", [P, BLOCKS])

        x_r = ring("x", 4, [P, BLOCKS, D])
        ctx_r = ring("ctx", 2, [P, BLOCKS, D])
        narrow_r = ring("narrow", 12, [P, CHUNK])
        wide_r = ring("wide", 6, [P, HALVES, CHUNK])
        xc2_r = ring("xc2", 1, [P, HALVES, CHUNK])
        gate_z_r = ring("gate_z", 2, [P, BLOCKS, INNER])
        skip_r = ring("skip", 2, [P, HALVES, CHUNK])
        bc_parts_r = ring("bc_parts", 1, [P, BLOCKS, PARTS, 2 * STATES], BF16)
        bc_rest_r = ring("bc_rest", 1, [P, BLOCKS, 2 * STATES])
        dt_low_r = ring("dt_low", 1, [P, BLOCKS, DT_RANK])
        bcT_r = ring("bcT", 2, [PARTS * 2 * STATES, CHUNK], BF16)
        delta_r = ring("delta", 2, [P, HALVES, CHUNK])
        dx_r = ring("dx", 2, [P, HALVES, CHUNK])

        decay_r = ring("decay", 3, [P, HALVES, CHUNK])
        drive_r = ring("drive", 2, [P, HALVES, CHUNK])
        state_r = ring("state", 2, [P, HALVES, CHUNK])
        c_r = ring("c_all", 2, [P, CHUNK])
        read_r = ring("read", 3, [P, HALVES, CHUNK])

        k_r, v_r = ring("k", 1, [P, CHUNK]), ring("v", 1, [P, CHUNK])
        x2_r = ring("x2", 2, [P, CHUNK])
        stats_r = ring("stats", 3, [P, BLOCKS, 6])
        moments_r = ring("moments", 3, [P, BLOCKS, 2])
        var_eps_r = ring("var_eps", 3, [P, BLOCKS])
        rstd_r = ring("rstd", 3, [P, BLOCKS])

        x2T_r = ring("x2T", 1, [P, CHUNK])
        logits_r = ring("logits", 1, [P, BLOCKS, EXPERTS])
        top_r = ring("top", 1, [P, BLOCKS, 8])
        top_at_r = ring("top_at", 1, [P, BLOCKS, 8], U32)
        top_f_r = ring("top_f", 1, [P, BLOCKS, 2])
        soft_r = ring("soft", 1, [P, 4, BLOCKS])
        comb_r = ring("comb", 1, [P, 3, BLOCKS, EXPERTS])
        comb_parts_r = ring("comb_parts", 1, [P, BLOCKS, PARTS, EXPERTS], BF16)
        comb_rest_r = ring("comb_rest", 1, [P, BLOCKS, EXPERTS])
        combT_r = ring("combT", 1, [PARTS * EXPERTS, CHUNK], BF16)
        comb_all_r = ring("comb_all", 2, [P, CHUNK])
        gu_r = ring("gu", 2, [P, CHUNK])
        hid_r = ring("hid", 2, [P, CHUNK])

        s = {n: sig(n) for n in (
            "consts", "setup_act", "setup_dve", "setup_pe", "setup_pool",
            "xT_mm", "xT", "xb_mm", "conv_bias", "conv_taps", "z_mm", "z_tanh", "gate_z", "conv_tanh", "xc2", "skip",
            "proj_mm", "dt_low", "bc_split", "bcT_mm", "bcT", "dt_lowT_mm", "dt_lowT", "dt_mm", "dt_pre",
            "dt_e", "dt_ln", "dt_dve", "delta", "dx",
            "decay", "c_mm", "c_all", "b_mm", "drive", "state", "read", "y_acc",
            "y_gated", "y_gatedT_mm", "y_gatedT", "out_mm", "sum", "stats", "moments", "var_eps", "rstd", "normed",
            "ctxT_mm", "ctxT", "x1T_mm", "x1T", "q_mm", "q_rot", "q", "k_mm", "k_rot", "k", "v_mm", "v", "score_mm", "ret",
            "retout_mm",
            "x2T_mm", "x2T", "router_mm", "router", "top_exp", "comb_split", "combT_mm", "combT", "comb_mm", "comb_all",
            "gu_mm", "g_tanh", "g_silu", "gu", "hid", "down_mm")}
        for name, count, r in (("x_load", 4, x_r), ("ctx_load", 2, ctx_r)):
            for i in range(count):
                r.free[i].landed = sig(f"{name}{i}")
        s_store = [sig(f"store{i}") for i in range(2)]

        x_view = io["x"].rearrange("b t d -> (b t) d").rearrange("(c q p) d -> c p q d", p=P, q=BLOCKS)
        ctx_view = io["ctx_1024"].rearrange("b t d -> (b t) d").rearrange("(c q p) d -> c p q d", p=P, q=BLOCKS)
        out_view = out_dram.rearrange("b t d -> (b t) d").rearrange("(c q p) d -> c p q d", p=P, q=BLOCKS)

        def load(r, view, c):
            slot = r.take(sync)
            slot.loaded = sync.load(slot.t[:, :, :], view[c], slot.landed)
            return slot

        x_in = {0: load(x_r, x_view, 0)}

        def const(dst, src):
            return sync.load(dst, src, s["consts"])

        def per_channel(dst, vector):
            for h in range(HALVES):
                const(dst[:, h:h + 1], vector[h * P:(h + 1) * P].rearrange("(p a) -> p a", a=1))

        const(ident[:, :], io["c_ident"])
        const(w_in[:, :], io["L0_attn_W_in"])
        const(conv_w[:, :, :], io["L0_attn_conv_w"].rearrange("(h p) k -> p h k", p=P))
        per_channel(conv_b, io["L0_attn_conv_b"])
        const(w_xproj[:, :, :], io["L0_attn_W_xproj"].rearrange("(h p) n -> p h n", p=P))
        const(w_dt[:, :], io["L0_attn_W_dt"])
        per_channel(b_dt, io["L0_attn_b_dt"])
        const(a_log[:, :, :], io["L0_attn_A_log"].rearrange("(h p) n -> p h n", p=P))
        per_channel(d_param, io["L0_attn_D_param"])
        const(pick_bc_rows[:, :], io["c_pick_bc"])
        const(pick_expert_rows[:, :], io["c_pick_expert"])
        const(w_out[:, :, :], io["L0_attn_W_out"].rearrange("(h p) n -> p h n", p=P))
        qkv_rows = [slot.whole for slot in narrow_r.free[0:3]]
        for rows_at, name in zip(qkv_rows, ("Wq", "Wk", "Wv")):
            const(rows_at[:, 0:D], io["L0_xattn_" + name])
        const(xpos[:, :, :], io["c_xpos"])
        const(decay_mask[:, :], io["c_decay_mask"])
        const(router_rows[:, :], io["L0_ffn_router_w"])
        const(router_bias[:, :], io["L0_ffn_router_bias"].rearrange("(a n) -> a n", a=1).partition_broadcast(P))
        const(expert_no[:, :], io["c_expert_no"])
        const(shared_rows[:, 0, :], io["L0_ffn_sh_gate"])
        const(shared_rows[:, 1, :], io["L0_ffn_sh_up"])
        const(shared_rows[:, 2, :], io["L0_ffn_sh_down"])
        const(gate_w[:, :, :], io["L0_ffn_gate_proj"].rearrange("k d e -> d k e"))
        const(up_w[:, :, :], io["L0_ffn_up_proj"].rearrange("k d e -> d k e"))
        landed = const(down_w[:, :, :], io["L0_ffn_down_proj"].rearrange("k e d -> (k e) d")
                     .rearrange("(j p) d -> p j d", p=P))
        weights_in = landed
        landed[0].times[landed[1]] = 22000.0

        for queue in (act, dve, pool, pe):
            queue.wait(weights_in)
        dve.copy(ident16[:, :], ident[:, :], s["setup_dve"])
        dve.ts(w_xproj_half[:, :, :], w_xproj[:, :, :], 0.5, 1.0, ALU.mult, ALU.mult, s["setup_dve"])
        dve.copy(pick_bc[:, :, :], pick_bc_rows[:, :].unsqueeze(2).to_broadcast([PARTS * 2 * STATES, 2 * STATES, P]),
                 s["setup_dve"])
        for slot in decay_r.free:
            zero_decay = dve.fill(slot.whole[:, :, :].rearrange("p h (b t) -> p (h b) t", t=T)[:, :, 0:1], 0.0,
                                  s["setup_dve"])
        a_exp_done = act.act(a_exp[:, :, :], a_log[:, :, :], ACT.Exp, s["setup_act"])
        dve.wait(a_exp_done)
        setup_dve = dve.ts(a_neg[:, :, :], a_exp[:, :, :], -1.0, 1.0, ALU.mult, ALU.mult, s["setup_dve"])
        pool.copy(pick_expert[:, :, :],
                  pick_expert_rows[:, :].unsqueeze(2).to_broadcast([PARTS * EXPERTS, EXPERTS, EXPERT_DIM]),
                  s["setup_pool"])
        setup_pool = pool.fill(minus_half[:, :], -0.5, s["setup_pool"])
        bank = banks.take(pe)
        for i in range(3):
            pe.transpose(bank.t[:, i * P:(i + 1) * P], shared_rows[:, i, :], ident[:, :])
        flipped = pe.transpose(bank.t[:, 3 * P:3 * P + EXPERTS], router_rows[:, :], ident[0:EXPERTS, 0:EXPERTS],
                               signal=s["setup_pe"])
        act.wait(flipped)
        act.act(shared_w[:, :, :], bank.t[:, 0:3 * P].rearrange("p (i n) -> p i n", i=3), ACT.Copy, s["setup_act"])
        setup_act = act.act(w_router[:, :], bank.t[:, 3 * P:3 * P + EXPERTS], ACT.Copy, s["setup_act"])
        bank.release(setup_act)
        bank = banks.take(pe)
        for i in range(3):
            flipped = pe.transpose(bank.t[:, i * P:(i + 1) * P], qkv_rows[i][:, 0:D], ident[:, :],
                                   signal=s["setup_pe"])
        act.wait(flipped)
        for i, w in enumerate((w_q, w_k, w_v)):
            qkv_done = act.act(w[:, :], bank.t[:, i * P:(i + 1) * P], ACT.Copy, s["setup_act"])
        bank.release(qkv_done)
        dve.wait(qkv_done)
        for w, swapped in ((w_q, w_q_swap), (w_k, w_k_swap)):
            from_pairs, to_pairs = (a[:, :].rearrange("p (n two) -> p n two", two=2) for a in (w, swapped))
            for i in (0, 1):
                setup_dve = dve.copy(to_pairs[:, :, i], from_pairs[:, :, 1 - i], s["setup_dve"])
        setup_act = qkv_done
        for slot in narrow_r.free[0:3]:
            slot.readers = [flipped]
        for queue in (pe, act, dve, pool):
            queue.wait(setup_dve, setup_act, setup_pool)

        def seqs(ap):
            return ap.rearrange("p (b t) -> p b t", t=T)

        def blocks(ap):
            return ap.rearrange("p (q n) -> p q n", q=BLOCKS)

        xT_of, prepared, gates = {}, {}, {}
        decays, c_alls, b_alls, drives, states, reads, scanned = {}, {}, {}, {}, {}, {}, {}
        contexts, attended, routed, weights_of, pairs, products, hidden, stores = {}, {}, {}, {}, {}, {}, {}, {}

        def got(table, key):
            while key not in table:
                yield NOT_YET
            return table[key]

        def prepare():
            for c in range(CHUNKS):
                if c + 1 < CHUNKS:
                    yield on(sync, takes=(x_r,))
                    x_in[c + 1] = load(x_r, x_view, c + 1)
                x = x_in[c]
                yield on(pe, x.loaded, takes=(banks,))
                bank = banks.take(pe)
                pe.wait(x.loaded)
                for q in range(BLOCKS):
                    flipped = pe.transpose(bank.t[:, q * P:(q + 1) * P], x.t[:, q, :], ident[:, :],
                                           signal=s["xT_mm"] if q == BLOCKS - 1 else None)
                yield on(act, flipped, takes=(narrow_r,))
                xT = narrow_r.take(act)
                act.wait(flipped)
                xT_done = act.act(xT.t[:, :], bank.t[:, :], ACT.Copy, s["xT"])
                bank.release(xT_done)
                xT_of[c] = (xT, xT_done)
                yield on(act, takes=(wide_r,))
                conv = wide_r.take(act)
                for h in range(HALVES):
                    yield on(pe, xT_done, takes=(banks,))
                    bank = banks.take(pe)
                    pe.wait(xT_done)
                    xb_done = pe.matmul(bank.t[:, :], w_in[:, h * P:(h + 1) * P], xT.t[:, :], signal=s["xb_mm"])
                    yield on(act, xb_done)
                    act.wait(xb_done)
                    tap = act.act(conv.t[:, h, :], bank.t[:, :], ACT.Identity, s["conv_bias"],
                                  bias=conv_b[:, h:h + 1], scale=conv_w[:, h, TAPS - 1:TAPS])
                    for k in range(1, TAPS):
                        yield on(dve, tap)
                        dve.wait(tap)
                        late_out = seqs(conv.t[:, h, :])[:, :, k:T]
                        tap = dve.stt(late_out, seqs(bank.t[:, :])[:, :, 0:T - k],
                                      conv_w[:, h, TAPS - 1 - k:TAPS - k], late_out, ALU.mult, ALU.add,
                                      s["conv_taps"])
                    bank.release(tap)
                xT.readers_of_conv = xb_done
                yield on(act, tap, takes=(wide_r,))
                conv_tanh = wide_r.take(act)
                act.wait(tap)
                tanh_done = act.act(conv_tanh.t[:, :, :], conv.t[:, :, :], ACT.Tanh, s["conv_tanh"], scale=0.5)
                yield on(dve, tanh_done, takes=(xc2_r,))
                xc2 = xc2_r.take(dve)
                dve.wait(tanh_done)
                xc2_done = dve.stt(xc2.t[:, :, :], conv_tanh.t[:, :, :], 1.0, conv.t[:, :, :], ALU.add, ALU.mult,
                                   s["xc2"])
                conv.release(xc2_done)
                conv_tanh.release(xc2_done)
                yield on(pe, xc2_done, takes=(banks,))
                bank = banks.take(pe)
                pe.wait(xc2_done)
                proj = bank.t[:, 0:BLOCKS * (DT_RANK + 2 * STATES)].rearrange("p (q n) -> p q n", q=BLOCKS)
                for q in range(BLOCKS):
                    for h in range(HALVES):
                        proj_done = pe.matmul(proj[:, q, :], xc2.t[:, h, q * P:(q + 1) * P], w_xproj_half[:, h, :],
                                              start=h == 0, stop=h == HALVES - 1,
                                              signal=s["proj_mm"] if (q, h) == (BLOCKS - 1, HALVES - 1) else None)
                yield on(dve, proj_done, takes=(bc_parts_r, bc_rest_r))
                parts, rest = bc_parts_r.take(dve), bc_rest_r.take(dve)
                bc = proj[:, :, DT_RANK:]
                dve.wait(proj_done)
                done = dve.copy(parts.t[:, :, 0, :], bc, s["bc_split"])
                yield on(dve, done)
                dve.wait(done)
                rest_done = dve.tt(rest.t[:, :, :], bc, parts.t[:, :, 0, :], ALU.subtract, s["bc_split"])
                yield on(dve, rest_done)
                dve.wait(rest_done)
                done = dve.copy(parts.t[:, :, 1, :], rest.t[:, :, :], s["bc_split"])
                yield on(dve, done)
                dve.wait(done)
                split_done = dve.tt(parts.t[:, :, 2, :], rest.t[:, :, :], parts.t[:, :, 1, :], ALU.subtract,
                                    s["bc_split"])
                rest.release(split_done)
                yield on(act, rest_done, takes=(dt_low_r,))
                dt_low = dt_low_r.take(act)
                act.wait(rest_done)
                low_done = act.act(dt_low.t[:, :, :], proj[:, :, 0:DT_RANK], ACT.Copy, s["dt_low"])
                bank.release(low_done)
                yield on(pe, low_done, takes=(banks,))
                bank = banks.take(pe)
                pe.wait(low_done)
                for q in range(BLOCKS):
                    flipped = pe.transpose(bank.t[0:DT_RANK, q * P:(q + 1) * P], dt_low.t[:, q, :], ident[:, :],
                                           signal=s["dt_lowT_mm"] if q == BLOCKS - 1 else None)
                dt_low.release(flipped)
                yield on(act, flipped, takes=(narrow_r,))
                dt_lowT = narrow_r.take(act)
                act.wait(flipped)
                lowT_done = act.act(dt_lowT.t[0:DT_RANK, :], bank.t[0:DT_RANK, :], ACT.Copy, s["dt_lowT"])
                bank.release(lowT_done)
                yield on(pe, split_done, takes=(banks,))
                bank = banks.take(pe)
                rows = PARTS * 2 * STATES
                bcT_bank = bank.t[:, :].bitcast(BF16)[0:rows, 0:CHUNK]
                pe.wait(split_done)
                for q in range(BLOCKS):
                    flipped = pe.transpose(bcT_bank[:, q * P:(q + 1) * P],
                                           parts.t[:, q, :, :].rearrange("p a n -> p (a n)"), ident16[:, :],
                                           signal=s["bcT_mm"] if q == BLOCKS - 1 else None)
                parts.release(flipped)
                yield on(act, flipped, takes=(bcT_r,))
                bcT = bcT_r.take(act)
                act.wait(flipped)
                bcT_done = act.act(bcT.t[:, :], bcT_bank, ACT.Copy, s["bcT"])
                bank.release(bcT_done)
                yield on(act, takes=(wide_r, wide_r))
                dt_abs, dt_relu = wide_r.take(act), wide_r.take(act)
                for h in range(HALVES):
                    yield on(pe, lowT_done, takes=(banks,))
                    bank = banks.take(pe)
                    pe.wait(lowT_done)
                    dt_done = pe.matmul(bank.t[:, :], w_dt[:, h * P:(h + 1) * P], dt_lowT.t[0:DT_RANK, :],
                                        signal=s["dt_mm"])
                    yield on(act, dt_done)
                    act.wait(dt_done)
                    act.act(dt_abs.t[:, h, :], bank.t[:, :], ACT.Abs, s["dt_pre"], bias=b_dt[:, h:h + 1])
                    pre_done = act.act(dt_relu.t[:, h, :], bank.t[:, :], ACT.Relu, s["dt_pre"], bias=b_dt[:, h:h + 1])
                    bank.release(pre_done)
                dt_lowT.release(dt_done)
                yield on(act, pre_done, takes=(wide_r,))
                dt_e = wide_r.take(act)
                act.wait(pre_done)
                e_done = act.act(dt_e.t[:, :, :], dt_abs.t[:, :, :], ACT.Exp, s["dt_e"], scale=-1.0)
                yield on(act, e_done)
                act.wait(e_done)
                dt_ln = dt_abs
                ln_done = act.act(dt_ln.t[:, :, :], dt_e.t[:, :, :], ACT.Ln, s["dt_ln"], bias=1.0)
                yield on(dve, e_done, takes=(wide_r,))
                dt_w = wide_r.take(dve)
                dve.wait(e_done)
                done = dve.ts(dt_w.t[:, :, :], dt_e.t[:, :, :], 1.0, -1.0, ALU.add, ALU.add, s["dt_dve"])
                yield on(dve, done)
                dve.wait(done)
                residue = dve.stt(dt_w.t[:, :, :], dt_w.t[:, :, :], -1.0, dt_e.t[:, :, :], ALU.mult, ALU.add,
                                  s["dt_dve"])
                dt_e.release(ln_done, residue)
                yield on(pool, residue, ln_done)
                pool.wait(residue, ln_done)
                log1p = pool.tt(dt_ln.t[:, :, :], dt_ln.t[:, :, :], dt_w.t[:, :, :], ALU.add, s["delta"])
                dt_w.release(log1p)
                yield on(pool, log1p, takes=(delta_r,))
                delta = delta_r.take(pool)
                pool.wait(log1p)
                delta_done = pool.tt(delta.t[:, :, :], dt_ln.t[:, :, :], dt_relu.t[:, :, :], ALU.add, s["delta"])
                dt_ln.release(delta_done)
                dt_relu.release(delta_done)
                yield on(dve, delta_done, takes=(dx_r,))
                dx = dx_r.take(dve)
                dve.wait(delta_done)
                dx_done = dve.stt(dx.t[:, :, :], xc2.t[:, :, :], 0.5, delta.t[:, :, :], ALU.mult, ALU.mult, s["dx"])
                prepared[c] = dict(delta=delta, dx=dx, bcT=bcT, delta_done=delta_done, dx_done=dx_done,
                                   bcT_done=bcT_done)
                yield on(dve, xc2_done, takes=(skip_r,))
                skip = skip_r.take(dve)
                dve.wait(xc2_done)
                for h in range(HALVES):
                    skip_done = dve.ts(skip.t[:, h, :], xc2.t[:, h, :], d_param[:, h:h + 1], 0.5, ALU.mult, ALU.mult,
                                       s["skip"])
                xc2.release(skip_done, proj_done)
                prepared[c].update(skip=skip, skip_done=skip_done)

        def gate():
            for c in range(CHUNKS):
                xT, xT_done = yield from got(xT_of, c)
                yield on(dve, takes=(gate_z_r,))
                gate_z = gate_z_r.take(dve)
                for g in range(2):
                    yield on(pe, xT_done, takes=(banks,))
                    bank = banks.take(pe)
                    pe.wait(xT_done)
                    for q in (0, 1):
                        block = 2 * g + q
                        z_done = pe.matmul(bank.t[:, q * INNER:(q + 1) * INNER], xT.t[:, block * P:(block + 1) * P],
                                           w_in[:, INNER:2 * INNER], signal=s["z_mm"] if q else None)
                    yield on(act, z_done, takes=(narrow_r,))
                    z_tanh = narrow_r.take(act)
                    act.wait(z_done)
                    tanh_done = act.act(z_tanh.t[:, :], bank.t[:, :], ACT.Tanh, s["z_tanh"], scale=0.5)
                    yield on(dve, tanh_done)
                    dve.wait(tanh_done)
                    gate_done = dve.stt(gate_z.t[:, 2 * g:2 * g + 2, :].rearrange("p q n -> p (q n)"),
                                        z_tanh.t[:, :], 1.0, bank.t[:, :], ALU.add, ALU.mult, s["gate_z"])
                    bank.release(gate_done)
                    z_tanh.release(gate_done)
                while c not in prepared:
                    yield NOT_YET
                xT.release(z_done, xT.readers_of_conv)
                gates[c] = (gate_z, gate_done)

        STEPS = CHUNKS * STATES

        def decay():
            for k in range(STEPS):
                c, n = divmod(k, STATES)
                p = yield from got(prepared, c)
                yield on(act, p["delta_done"], takes=(decay_r,))
                slot = decay_r.take(act)
                act.wait(p["delta_done"])
                for h in range(HALVES):
                    done = act.act(seqs(slot.t[:, h, :])[:, :, 1:T], seqs(p["delta"].t[:, h, :])[:, :, 1:T], ACT.Exp,
                                   s["decay"], scale=a_neg[:, h, n:n + 1])
                decays[k] = (slot, done)
                if n == STATES - 1:
                    p["delta"].release(done, p["dx_done"])

        def spread_c():
            for k in range(STEPS):
                c, n = divmod(k, STATES)
                p = yield from got(prepared, c)
                yield on(pe, p["bcT_done"], takes=(banks, c_r))
                bank = banks.take(pe)
                slot = c_r.take(act)
                pe.wait(p["bcT_done"])
                c_mm = pe.matmul(bank.t[:, :], pick_bc[:, STATES + n, :], p["bcT"].t[:, :], signal=s["c_mm"])
                yield on(act, c_mm)
                act.wait(c_mm)
                copied = act.act(slot.t[:, :], bank.t[:, :], ACT.Copy, s["c_all"])
                bank.release(copied)
                c_alls[k] = (slot, copied)
                if n == STATES - 1:
                    p["c_spread"] = c_mm

        def spread_b():
            for k in range(STEPS):
                c, n = divmod(k, STATES)
                p = yield from got(prepared, c)
                yield on(pe, p["bcT_done"], takes=(b_bank,))
                bank = b_bank.take(pe)
                pe.wait(p["bcT_done"])
                done = pe.matmul(bank.t[:, :], pick_bc[:, n, :], p["bcT"].t[:, :], signal=s["b_mm"])
                b_alls[k] = (bank, done)
                if n == STATES - 1:
                    c_mm = yield from got(p, "c_spread")
                    p["bcT"].release(done, c_mm)

        def drive():
            for k in range(STEPS):
                c, n = divmod(k, STATES)
                bank, spread = yield from got(b_alls, k)
                p = prepared[c]
                yield on(dve, p["dx_done"], spread, takes=(drive_r,))
                slot = drive_r.take(dve)
                dve.wait(p["dx_done"], spread)
                done = dve.tt(slot.t[:, :, :], p["dx"].t[:, :, :],
                              bank.t[:, :].unsqueeze(1).to_broadcast([P, HALVES, CHUNK]), ALU.mult, s["drive"])
                bank.release(done)
                drives[k] = (slot, done)
                if n == STATES - 1:
                    p["dx"].release(done)

        def scan():
            flat = "p h n -> p (h n)"
            for k in range(STEPS):
                decay_slot, decay_done = yield from got(decays, k)
                drive_slot, drive_done = yield from got(drives, k)
                yield on(dve, decay_done, drive_done, takes=(state_r,))
                slot = state_r.take(dve)
                dve.wait(decay_done, drive_done)
                done = dve.scan(*(x.t[:, :, :].rearrange(flat) for x in (slot, decay_slot, drive_slot)), s["state"])
                decay_slot.release(done)
                drive_slot.release(done)
                states[k] = (slot, done)

        def read():
            for k in range(STEPS):
                state, scan_done = yield from got(states, k)
                c_all, copied = yield from got(c_alls, k)
                yield on(pool, scan_done, copied, takes=(read_r,))
                slot = read_r.take(pool)
                pool.wait(scan_done, copied)
                done = pool.tt(slot.t[:, :, :], state.t[:, :, :],
                               c_all.t[:, :].unsqueeze(1).to_broadcast([P, HALVES, CHUNK]), ALU.mult, s["read"])
                state.release(done)
                c_all.release(done)
                reads[k] = (slot, done)

        def sum_states():
            for k in range(STEPS):
                c, n = divmod(k, STATES)
                slot, read_done = yield from got(reads, k)
                if n == 0:
                    yield on(pe, read_done, takes=(y_banks,))
                    y = y_banks.take(pe)
                else:
                    yield on(pe, read_done)
                pe.wait(read_done)
                for q in range(BLOCKS):
                    for h in range(HALVES):
                        done = pe.transpose(y.t[:, q, h * P:(h + 1) * P], slot.t[:, h, q * P:(q + 1) * P],
                                            ident[:, :], start=(n == 0 and h == 0 and q % 2 == 0), stop=False,
                                            signal=s["y_acc"] if (q, h) == (BLOCKS - 1, HALVES - 1) else None)
                slot.release(done)
                if n == STATES - 1:
                    p = prepared[c]
                    yield on(pe, p["skip_done"])
                    pe.wait(p["skip_done"])
                    for q in range(BLOCKS):
                        for h in range(HALVES):
                            done = pe.transpose(y.t[:, q, h * P:(h + 1) * P], p["skip"].t[:, h, q * P:(q + 1) * P],
                                                ident[:, :], start=False, stop=True,
                                                signal=s["y_acc"] if (q, h) == (BLOCKS - 1, HALVES - 1) else None)
                    p["skip"].release(done)
                    scanned[c] = (y, done)

        def normalise(total, total_done, out_ring):
            yield on(dve, total_done, takes=(stats_r, moments_r))
            stats, moments = stats_r.take(dve), moments_r.take(dve)
            dve.wait(total_done)
            for q in range(BLOCKS):
                done = dve.bn_stats(stats.t[:, q, :], total.t[:, q, :], s["stats"])
            yield on(dve, done)
            dve.wait(done)
            for q in range(BLOCKS):
                done = dve.bn_aggr(moments.t[:, q, :], stats.t[:, q, :], s["moments"])
            stats.release(done)
            yield on(pool, done, takes=(var_eps_r, rstd_r))
            var_eps, rstd = var_eps_r.take(pool), rstd_r.take(pool)
            pool.wait(done)
            eps_done = pool.ts(var_eps.t[:, :], moments.t[:, :, 1], LN_EPS, 1.0, ALU.add, ALU.mult, s["var_eps"])
            pool.wait(eps_done)
            rstd_done = pool.tt(rstd.t[:, :], var_eps.t[:, :], minus_half[:, :], ALU.pow, s["rstd"])
            var_eps.release(rstd_done)
            yield on(dve, rstd_done, takes=(out_ring,))
            out = out_ring.take(dve, blocks=True)
            dve.wait(rstd_done)
            for q in range(BLOCKS):
                done = dve.ts(out.t[:, q, :], total.t[:, q, :], moments.t[:, q, 0:1], rstd.t[:, q:q + 1],
                              ALU.subtract, ALU.mult, s["normed"])
            total.release(done)
            moments.release(done)
            rstd.release(done)
            return out, done

        def to_channels(src, src_done, bank_ring, out_ring, mm_signal, signal):
            yield on(pe, src_done, takes=(bank_ring,))
            bank = bank_ring.take(pe)
            pe.wait(src_done)
            for q in range(BLOCKS):
                flipped = pe.transpose(bank.t[:, q * P:(q + 1) * P], src[:, q, :], ident[:, :],
                                       signal=mm_signal if q == BLOCKS - 1 else None)
            yield on(act, flipped, takes=(out_ring,))
            out = out_ring.take(act)
            act.wait(flipped)
            copied = act.act(out.t[:, :], bank.t[:, :], ACT.Copy, signal)
            bank.release(copied)
            return out, flipped, copied

        def rotate(w, w_swap, src, src_done, table, out_ring, name):
            turned = []
            for i, weights in enumerate((w, w_swap)):
                yield on(pe, src_done, takes=(banks,))
                bank = banks.take(pe)
                pe.wait(src_done)
                mm_done = pe.matmul(bank.t[:, :], weights[:, :], src[:, :], signal=s[name + "_mm"])
                yield on(dve, mm_done, takes=(narrow_r,))
                rot = narrow_r.take(dve)
                dve.wait(mm_done)
                done = dve.tt(seqs(rot.t[:, :]), seqs(bank.t[:, :]),
                              xpos[:, 2 * table + i, :].unsqueeze(1).to_broadcast([P, CHUNK_SEQS, T]), ALU.mult,
                              s[name + "_rot"])
                bank.release(done)
                turned.append(rot)
            yield on(pool, done, takes=(out_ring,))
            out = out_ring.take(pool)
            pool.wait(done)
            added = pool.tt(out.t[:, :], turned[0].t[:, :], turned[1].t[:, :], ALU.add, s[name])
            for rot in turned:
                rot.release(added)
            return out, added, mm_done

        def context():
            for c in range(CHUNKS):
                yield on(sync, takes=(ctx_r,))
                slot = load(ctx_r, ctx_view, c)
                ctxT, ctx_mm, ctxT_done = yield from to_channels(slot.t, slot.loaded, banks, narrow_r, s["ctxT_mm"],
                                                                 s["ctxT"])
                slot.release(ctx_mm)
                k_t, k_done, mm = yield from rotate(w_k, w_k_swap, ctxT.t, ctxT_done, 1, k_r, "k")
                yield on(pe, takes=(banks,))
                bank = banks.take(pe)
                for q in range(BLOCKS):
                    mm = pe.matmul(bank.t[:, q * P:(q + 1) * P], ctxT.t[:, q * P:(q + 1) * P], w_v[:, :],
                                   signal=s["v_mm"] if q == BLOCKS - 1 else None)
                ctxT.release(mm)
                yield on(act, mm, takes=(v_r,))
                v = v_r.take(act, blocks=True)
                act.wait(mm)
                v_done = act.act(v.t[:, :, :], blocks(bank.t[:, :]), ACT.Copy, s["v"])
                bank.release(v_done)
                contexts[c] = (k_t, k_done, v, v_done)

        def attend():
            for c in range(CHUNKS):
                y, y_done = yield from got(scanned, c)
                gate_z, gate_done = yield from got(gates, c)
                yield on(dve, y_done, gate_done, takes=(wide_r,))
                y_gated = wide_r.take(dve)
                gated_y = y_gated.t[:, :, :].rearrange("p h n -> p (h n)").rearrange("p (q n) -> p q n", q=BLOCKS)
                dve.wait(y_done, gate_done)
                for g in range(2):
                    half = slice(2 * g, 2 * g + 2)
                    gated = dve.stt(gated_y[:, half, :], gate_z.t[:, half, :], 0.5, y.t[:, half, :], ALU.mult,
                                    ALU.mult, s["y_gated"])
                y.release(gated)
                gate_z.release(gated)
                yield on(act, takes=(wide_r,))
                y_gatedT = wide_r.take(act)
                for h in range(HALVES):
                    yield on(pe, gated, takes=(banks,))
                    bank = banks.take(pe)
                    pe.wait(gated)
                    for q in range(BLOCKS):
                        flipped = pe.transpose(bank.t[:, q * P:(q + 1) * P], gated_y[:, q, h * P:(h + 1) * P],
                                               ident[:, :], signal=s["y_gatedT_mm"] if q == BLOCKS - 1 else None)
                    yield on(act, flipped)
                    act.wait(flipped)
                    copied = act.act(y_gatedT.t[:, h, :], bank.t[:, :], ACT.Copy, s["y_gatedT"])
                    bank.release(copied)
                y_gated.release(flipped)
                yield on(pe, copied, takes=(banks,))
                bank = banks.take(pe)
                pe.wait(copied)
                for q in range(BLOCKS):
                    for h in range(HALVES):
                        mm = pe.matmul(bank.t[:, q * P:(q + 1) * P], y_gatedT.t[:, h, q * P:(q + 1) * P],
                                       w_out[:, h, :], start=h == 0, stop=h == HALVES - 1,
                                       signal=s["out_mm"] if (q, h) == (BLOCKS - 1, HALVES - 1) else None)
                y_gatedT.release(mm)
                yield on(dve, mm, takes=(narrow_r,))
                total = narrow_r.take(dve, blocks=True)
                dve.wait(mm)
                x = x_in.pop(c)
                done = dve.tt(total.t[:, :, :], blocks(bank.t[:, :]), x.t[:, :, :], ALU.add, s["sum"])
                bank.release(done)
                x.release(done)
                x1, x1_done = yield from normalise(total, done, narrow_r)
                x1T, x1T_mm, x1T_done = yield from to_channels(x1.t, x1_done, banks, narrow_r, s["x1T_mm"], s["x1T"])
                q_t, q_done, mm = yield from rotate(w_q, w_q_swap, x1T.t, x1T_done, 0, narrow_r, "q")
                x1T.release(mm)
                k_t, k_done, v, v_done = yield from got(contexts, c)
                yield on(pe, q_done, k_done, takes=(banks,))
                bank = banks.take(pe)
                pe.wait(q_done, k_done)
                for q in range(BLOCKS):
                    cols = slice(q * P, (q + 1) * P)
                    mm = pe.matmul(bank.t[:, cols], k_t.t[:, cols], q_t.t[:, cols],
                                   signal=s["score_mm"] if q == BLOCKS - 1 else None)
                k_t.release(mm)
                q_t.release(mm)
                yield on(dve, mm, takes=(narrow_r,))
                ret = narrow_r.take(dve, blocks=True)
                dve.wait(mm)
                ret_done = dve.tt(ret.t[:, :, :], blocks(bank.t[:, :]),
                                  decay_mask[:, :].unsqueeze(1).to_broadcast([P, BLOCKS, P]), ALU.mult, s["ret"])
                bank.release(ret_done)
                yield on(pe, ret_done, v_done, takes=(banks,))
                bank = banks.take(pe)
                pe.wait(ret_done, v_done)
                for q in range(BLOCKS):
                    mm = pe.matmul(bank.t[:, q * P:(q + 1) * P], ret.t[:, q, :], v.t[:, q, :],
                                   signal=s["retout_mm"] if q == BLOCKS - 1 else None)
                ret.release(mm)
                v.release(mm)
                yield on(dve, mm, takes=(narrow_r,))
                total = narrow_r.take(dve, blocks=True)
                dve.wait(mm)
                done = dve.tt(total.t[:, :, :], blocks(bank.t[:, :]), x1.t[:, :, :], ALU.add, s["sum"])
                bank.release(done)
                x1.release(done, x1T_mm)
                attended[c] = yield from normalise(total, done, x2_r)

        def route():
            for c in range(CHUNKS):
                x2, x2_done = yield from got(attended, c)
                x2T, x2T_mm, x2T_done = yield from to_channels(x2.t, x2_done, banks, x2T_r, s["x2T_mm"], s["x2T"])
                yield on(pe, x2T_done, takes=(banks,))
                bank = banks.take(pe)
                pe.wait(x2T_done)
                scores = bank.t[:, 0:BLOCKS * EXPERTS].rearrange("p (q n) -> p q n", q=BLOCKS)
                for q in range(BLOCKS):
                    mm = pe.matmul(scores[:, q, :], x2T.t[:, q * P:(q + 1) * P], w_router[:, :],
                                   signal=s["router_mm"] if q == BLOCKS - 1 else None)
                routed[c] = (x2, x2T, x2T_mm, x2T_done, mm)
                shape = [P, BLOCKS, EXPERTS]
                yield on(dve, mm, takes=(logits_r,))
                logits = logits_r.take(dve)
                dve.wait(mm)
                done = dve.tt(logits.t[:, :, :], scores, router_bias[:, :].unsqueeze(1).to_broadcast(shape), ALU.add,
                              s["router"])
                bank.release(done)
                yield on(dve, done, takes=(top_r, top_at_r))
                top, top_at = top_r.take(dve), top_at_r.take(dve)
                dve.wait(done)
                for q in range(BLOCKS):
                    done = dve.max8(top.t[:, q, :], logits.t[:, q, :], s["router"])
                yield on(dve, done)
                dve.wait(done)
                for q in range(BLOCKS):
                    at_done = dve.max8_index(top_at.t[:, q, :], top.t[:, q, :], logits.t[:, q, :], s["router"])
                logits.release(at_done)
                yield on(dve, at_done, takes=(soft_r, top_f_r))
                soft, top_f = soft_r.take(dve), top_f_r.take(dve)
                dve.wait(at_done)
                done = dve.tt(soft.t[:, 0, :], top.t[:, :, 1], top.t[:, :, 0], ALU.subtract, s["router"])
                f_done = dve.copy(top_f.t[:, :, :], top_at.t[:, :, 0:2], s["router"])
                top.release(done)
                top_at.release(f_done)
                yield on(act, done)
                act.wait(done)
                e_done = act.act(soft.t[:, 1, :], soft.t[:, 0, :], ACT.Exp, s["top_exp"])
                yield on(dve, e_done)
                dve.wait(e_done)
                done = dve.ts(soft.t[:, 0, :], soft.t[:, 1, :], 1.0, 1.0, ALU.add, ALU.mult, s["router"])
                yield on(dve, done)
                dve.wait(done)
                done = dve.reciprocal(soft.t[:, 2, :], soft.t[:, 0, :], s["router"])
                yield on(dve, done)
                dve.wait(done)
                p2_done = dve.tt(soft.t[:, 3, :], soft.t[:, 1, :], soft.t[:, 2, :], ALU.mult, s["router"])
                yield on(dve, f_done, takes=(comb_r,))
                comb = comb_r.take(dve)
                dve.wait(f_done)
                for i in (0, 1):
                    eq = dve.tt(comb.t[:, i, :, :], expert_no[:, :].unsqueeze(1).to_broadcast(shape),
                                top_f.t[:, :, i].unsqueeze(2).to_broadcast(shape), ALU.is_equal, s["router"])
                yield on(dve, eq, p2_done)
                dve.wait(eq, p2_done)
                for i in (0, 1):
                    done = dve.tt(comb.t[:, i, :, :], comb.t[:, i, :, :],
                                  soft.t[:, 2 + i, :].unsqueeze(2).to_broadcast(shape), ALU.mult, s["router"])
                top_f.release(eq)
                soft.release(done)
                yield on(dve, done)
                dve.wait(done)
                done = dve.tt(comb.t[:, 2, :, :], comb.t[:, 0, :, :], comb.t[:, 1, :, :], ALU.add, s["router"])
                yield on(dve, done, takes=(comb_parts_r, comb_rest_r))
                parts, rest = comb_parts_r.take(dve), comb_rest_r.take(dve)
                whole = comb.t[:, 2, :, :]
                dve.wait(done)
                done = dve.copy(parts.t[:, :, 0, :], whole, s["comb_split"])
                yield on(dve, done)
                dve.wait(done)
                done = dve.tt(rest.t[:, :, :], whole, parts.t[:, :, 0, :], ALU.subtract, s["comb_split"])
                comb.release(done)
                yield on(dve, done)
                dve.wait(done)
                done = dve.copy(parts.t[:, :, 1, :], rest.t[:, :, :], s["comb_split"])
                yield on(dve, done)
                dve.wait(done)
                split_done = dve.tt(parts.t[:, :, 2, :], rest.t[:, :, :], parts.t[:, :, 1, :], ALU.subtract,
                                    s["comb_split"])
                rest.release(split_done)
                yield on(pe, split_done, takes=(banks,))
                bank = banks.take(pe)
                rows = PARTS * EXPERTS
                combT_bank = bank.t[:, :].bitcast(BF16)[0:rows, 0:CHUNK]
                pe.wait(split_done)
                for q in range(BLOCKS):
                    mm = pe.transpose(combT_bank[:, q * P:(q + 1) * P],
                                      parts.t[:, q, :, :].rearrange("p a n -> p (a n)"), ident16[:, :],
                                      signal=s["combT_mm"] if q == BLOCKS - 1 else None)
                parts.release(mm)
                yield on(act, mm, takes=(combT_r,))
                combT = combT_r.take(act)
                act.wait(mm)
                combT_done = act.act(combT.t[:, :], combT_bank, ACT.Copy, s["combT"])
                bank.release(combT_done)
                for j in range(PAIRS):
                    yield on(pe, combT_done, takes=(banks, comb_all_r))
                    bank = banks.take(pe)
                    slot = comb_all_r.take(act)
                    pe.wait(combT_done)
                    mm = pe.matmul(bank.t[:, :], pick_expert[:, 2 * j:2 * j + 2, :].rearrange("p k e -> p (k e)"),
                                   combT.t[:, :], signal=s["comb_mm"])
                    yield on(act, mm)
                    act.wait(mm)
                    copied = act.act(slot.t[:, :], bank.t[:, :], ACT.Copy, s["comb_all"])
                    bank.release(copied)
                    weights_of[c, j] = (slot, copied)
                combT.release(mm)

        TILES = [None] + list(range(PAIRS))

        def up_gate():
            for c in range(CHUNKS):
                x2, x2T, x2T_mm, x2T_done, router_mm = yield from got(routed, c)
                for j in TILES:
                    yield on(pe, x2T_done, takes=(banks, banks))
                    pe.wait(x2T_done)
                    pair = []
                    for i, w in enumerate((gate_w, up_w)):
                        lhsT = (shared_w[:, i, :] if j is None else
                                w[:, 2 * j:2 * j + 2, :].rearrange("p k e -> p (k e)"))
                        bank = banks.take(pe)
                        pair.append((bank, pe.matmul(bank.t[:, :], lhsT, x2T.t[:, :], signal=s["gu_mm"])))
                    pairs[c, j] = pair
                x2T.release(pair[1][1], router_mm)

        def activate():
            for c in range(CHUNKS):
                for j in TILES:
                    (g_bank, g_mm), (u_bank, u_mm) = yield from got(pairs, (c, j))
                    yield on(act, g_mm, takes=(narrow_r,))
                    g_tanh = narrow_r.take(act)
                    act.wait(g_mm)
                    tanh_done = act.act(g_tanh.t[:, :], g_bank.t[:, :], ACT.Tanh, s["g_tanh"], scale=0.5)
                    yield on(dve, tanh_done, takes=(narrow_r,))
                    g_silu = narrow_r.take(dve)
                    dve.wait(tanh_done)
                    silu_done = dve.stt(g_silu.t[:, :], g_tanh.t[:, :], 1.0, g_bank.t[:, :], ALU.add, ALU.mult,
                                        s["g_silu"])
                    g_bank.release(silu_done)
                    g_tanh.release(silu_done)
                    target_ring = hid_r if j is None else gu_r
                    yield on(dve, silu_done, u_mm, takes=(target_ring,))
                    target = target_ring.take(dve)
                    dve.wait(silu_done, u_mm)
                    done = dve.stt(target.t[:, :], g_silu.t[:, :], 0.5, u_bank.t[:, :], ALU.mult, ALU.mult, s["gu"])
                    u_bank.release(done)
                    g_silu.release(done)
                    (hidden if j is None else products)[c, j] = (target, done)

        def weigh():
            for c in range(CHUNKS):
                for j in range(PAIRS):
                    product, product_done = yield from got(products, (c, j))
                    weight, weight_done = yield from got(weights_of, (c, j))
                    yield on(pool, product_done, weight_done, takes=(hid_r,))
                    hid = hid_r.take(pool)
                    pool.wait(product_done, weight_done)
                    done = pool.tt(hid.t[:, :], product.t[:, :], weight.t[:, :], ALU.mult, s["hid"])
                    product.release(done)
                    weight.release(done)
                    hidden[c, j] = (hid, done)

        def down():
            for c in range(CHUNKS):
                for j in TILES:
                    hid, hid_done = yield from got(hidden, (c, j))
                    if j is None:
                        yield on(pe, hid_done, takes=(down_bank,))
                        bank = down_bank.take(pe)
                    else:
                        yield on(pe, hid_done)
                    pe.wait(hid_done)
                    w = shared_w[:, 2, :] if j is None else down_w[:, j, :]
                    for q in range(BLOCKS):
                        mm = pe.matmul(bank.t[:, q * P:(q + 1) * P], hid.t[:, q * P:(q + 1) * P], w,
                                       start=(j is None and q == 0), stop=j == PAIRS - 1,
                                       signal=s["down_mm"] if q == BLOCKS - 1 else None)
                    hid.release(mm)
                x2, x2T, x2T_mm, x2T_done, router_mm = routed[c]
                yield on(dve, mm, takes=(narrow_r,))
                total = narrow_r.take(dve, blocks=True)
                dve.wait(mm)
                done = dve.tt(total.t[:, :, :], blocks(bank.t[:, :]), x2.t[:, :, :], ALU.add, s["sum"])
                bank.release(done)
                x2.release(done, x2T_mm)
                y, y_done = yield from normalise(total, done, narrow_r)
                yield on(sync, y_done)
                sync.wait(y_done)
                stored = sync.load(out_view[c], y.t[:, :, :], s_store[c % 2])
                y.release(stored)
                stores[c % 2] = stored

        run([stream() for stream in (
            prepare, attend, route, gate, scan, drive, read, decay, spread_b, spread_c, sum_states, down, activate,
            up_gate, weigh, context)])
        sync.wait(*stores.values())

        block = ctx.enter_context(nc.Block())

        @block.sync
        def _(eng):
            sync.emit(eng)

        @block.tensor
        def _(eng):
            pe.emit(eng)

        @block.scalar
        def _(eng):
            act.emit(eng)

        @block.vector
        def _(eng):
            dve.emit(eng)

        @block.gpsimd
        def _(eng):
            pool.emit(eng)


def shape_constants(np):
    f = np.float32
    pos = np.arange(T, dtype=np.float64)
    base = (np.arange(0, D, 2, dtype=np.float64) + 0.4 * D) / (1.4 * D)
    freqs = 1.0 / 10000.0 ** (np.arange(D // 2, dtype=np.float64) / (D // 2))
    scale = base[:, None] ** (pos[None, :] / 512.0)
    angle = freqs[:, None] * pos[None, :]
    sign = np.where(np.arange(D) % 2 == 0, -1.0, 1.0)[:, None]
    tables = []
    for factor in (scale, 1.0 / scale):
        tables += [np.repeat(np.cos(angle) * factor, 2, axis=0), np.repeat(np.sin(angle) * factor, 2, axis=0) * sign]
    key, query = np.arange(P)[:, None], np.arange(P)[None, :]
    mask = np.where((key // T == query // T) & (query >= key), 0.96875 ** np.maximum(query - key, 0.0), 0.0)

    def picks(n):
        return (np.arange(PARTS * n)[:, None] % n == np.arange(n)[None, :]).astype(f)

    return {
        "c_ident": np.eye(P, dtype=f),
        "c_xpos": np.ascontiguousarray(np.stack(tables, axis=1)).astype(f),
        "c_decay_mask": mask.astype(f),
        "c_pick_bc": picks(2 * STATES),
        "c_pick_expert": picks(EXPERTS),
        "c_expert_no": np.tile(np.arange(EXPERTS, dtype=f), (P, 1)),
    }


def kernel(**inputs):
    import numpy as _np
    import concourse.bacc as _bacc
    from concourse import mybir as _mybir
    from concourse.bass_utils import run_bass_kernel_spmd as _run

    nc = _bacc.Bacc("TRN2", target_bir_lowering=False, num_devices=1)
    arrays, io = {}, {}
    given = {n: _np.ascontiguousarray(a) for n, a in inputs.items()}
    for name, a in list(given.items()) + list(shape_constants(_np).items()):
        arrays[f"in_{name}_dram"] = a
        io[name] = nc.dram_tensor(f"in_{name}_dram", a.shape, _mybir.dt.from_np(a.dtype), kind="ExternalInput").ap()
    out = nc.dram_tensor("out_0_dram", (SEQS, T, D), F32, kind="ExternalOutput").ap()
    decoder_layer(nc, io, out)
    r = _run(nc, [arrays], core_ids=[0])
    return r.results[0]["out_0_dram"]
```

```python
from contextlib import ExitStack

import concourse.bass as bass
from concourse import mybir

ALU = mybir.AluOpType
ACT = mybir.ActivationFunctionType
F32 = mybir.dt.float32
BF16 = mybir.dt.bfloat16
U32 = mybir.dt.uint32

P = 128
SEQS, T, D = 128, 64, 128
INNER = 2 * D
HALVES = INNER // P
STATES = 16
TAPS = 4
DT_RANK = 8
EXPERTS, EXPERT_DIM = 16, 64
CHUNK = 512
BLOCKS = CHUNK // P
CHUNKS = SEQS * T // CHUNK
CHUNK_SEQS = CHUNK // T
PAIRS = EXPERTS * EXPERT_DIM // P
PARTS = 3
LN_EPS = 1e-5

class Signal:

    def __init__(self, ctx, nc, name):
        self.name, self.sem, self.count, self.times = name, ctx.enter_context(nc.semaphore(name)), 0, {}

    def raised(self, by, time):
        self.count += by
        self.times[self.count] = time
        return (self, self.count)


def time_of(tokens):
    return max([signal.times[value] for signal, value in tokens], default=0.0)


class Slot:

    def __init__(self, ring, tensor):
        self.ring, self.whole, self.readers = ring, tensor, []

    def release(self, *tokens):
        self.readers = list(tokens)
        self.ring.free.append(self)


class Ring:

    def __init__(self, tensors):
        self.free = [Slot(self, t) for t in tensors]

    def take(self, queue, blocks=False):
        slot = self.free.pop(0)
        slot.t = slot.whole[:, :].rearrange("p (q n) -> p q n", q=BLOCKS) if blocks else slot.whole
        queue.wait(*slot.readers)
        return slot


class Queue:

    def __init__(self, first=0.0, each=0.0, pointer=0.0, sends=0.0, sees=0.0):
        self.ops, self.passed, self.clock = [], {}, 0.0
        self.first, self.each, self.pointer, self.sends, self.sees = first, each, pointer, sends, sees

    def wait(self, *tokens):
        for signal, value in tokens:
            self.clock = max(self.clock, signal.times[value] + self.sees)
            if self.passed.get(signal.name, 0) < value:
                self.passed[signal.name] = value
                self.ops.append(lambda e, s=signal.sem, v=value: e.wait_ge(s, v))

    def put(self, op, signal, out=None, by=1, length=None):
        if length is None:
            length = self.first + self.each * out.free_size()
        self.clock += length
        if signal is None:
            self.ops.append(op)
            return None
        self.ops.append(lambda e: op(e).then_inc(signal.sem, by))
        return signal.raised(by, self.clock + self.sends)

    def emit(self, engine):
        for op in self.ops:
            op(engine)

    def load(self, dst, src, signal):
        return self.put(lambda e: e.dma_start(dst, src), signal, by=16, length=60.0)

    def matmul(self, out, lhsT, rhs, start=True, stop=True, signal=None):
        passes = 4 if rhs.dtype == F32 else 1
        return self.put(lambda e: e.matmul(out, lhsT, rhs, start=start, stop=stop, skip_group_check=True), signal,
                        length=max(out.free_size(), 64) * passes * 0.42)

    def transpose(self, out, in_, identity, start=True, stop=True, signal=None):
        return self.put(lambda e: e.matmul(out, in_, identity, is_transpose=True, start=start, stop=stop,
                                           skip_group_check=True), signal, length=115.0)

    def act(self, out, in_, func, signal, bias=None, scale=1.0):
        pointers = sum(not isinstance(x, float) for x in (0.0 if bias is None else bias, scale))
        length = self.first + self.each * out.free_size() + self.pointer * pointers
        if bias is None:
            return self.put(lambda e: e.activation(out, in_, func, scale=scale), signal, length=length)
        return self.put(lambda e: e.activation(out, in_, func, bias=bias, scale=scale), signal, length=length)

    def copy(self, out, in_, signal):
        return self.put(lambda e: e.tensor_copy(out, in_), signal, out)

    def fill(self, out, value, signal):
        return self.put(lambda e: e.memset(out, value), signal, out)

    def reciprocal(self, out, in_, signal):
        return self.put(lambda e: e.reciprocal(out, in_), signal, out)

    def bn_stats(self, out, in_, signal):
        return self.put(lambda e: e.bn_stats(out, in_), signal, in_)

    def bn_aggr(self, out, in_, signal):
        return self.put(lambda e: e.bn_aggr(out, in_), signal, in_)

    def max8(self, out, in_, signal):
        return self.put(lambda e: e.max(out, in_), signal, in_)

    def max8_index(self, out, values, in_, signal):
        return self.put(lambda e: e.max_index(out, values, in_), signal, in_, length=200.0)

    def scan(self, out, factor, addend, signal):
        return self.put(lambda e: e.tensor_tensor_scan(out, factor, addend, 0.0, ALU.mult, ALU.add), signal, out)

    def tt(self, out, a, b, op, signal):
        return self.put(lambda e: e.tensor_tensor(out, a, b, op), signal,
                        length=self.first + self.each * out.free_size() + (800.0 if op is ALU.pow else 0.0))

    def ts(self, out, a, s1, s2, op0, op1, signal):
        return self.put(lambda e: e.tensor_scalar(out, a, s1, s2, op0, op1), signal,
                        length=self.first + self.each * out.free_size() / 2
                        + self.pointer * sum(not isinstance(x, float) for x in (s1, s2)))

    def stt(self, out, a, scalar, b, op0, op1, signal):
        return self.put(lambda e: e.scalar_tensor_tensor(out=out, in0=a, scalar=scalar, in1=b, op0=op0, op1=op1),
                        signal, out)


def on(queue, *tokens, takes=()):
    return queue, tokens, takes


def start_time(need):
    queue, tokens, takes = need
    at = max(queue.clock, time_of(tokens) + queue.sees)
    for ring in set(takes):
        count = takes.count(ring)
        if len(ring.free) < count:
            return None
        for slot in ring.free[:count]:
            at = max(at, time_of(slot.readers) + queue.sees)
    return at


def run(lags, reached):
    needs = {}
    for stream in lags:
        reached[stream] = 0.0
        needs[stream] = (stream(), NOT_YET)
    while needs:
        for stream, (steps, need) in list(needs.items()):
            if need[0] is None:
                need = next(steps, None)
                needs[stream] = (steps, need)
                if need is None:
                    del needs[stream]
        starts = {stream: start_time(need) for stream, (_, need) in needs.items() if need[0] is not None}
        starts = {stream: at for stream, at in starts.items() if at is not None}
        if not needs:
            return
        assert starts, "no stream can go on"
        first = min(starts, key=starts.get)
        queue, latest = needs[first][1][0], starts[first] + MARGIN
        chosen = min((s for s in starts if needs[s][1][0] is queue and starts[s] <= latest),
                     key=lambda s: reached[s] + lags[s])
        steps = needs[chosen][0]
        need = next(steps, None)
        needs[chosen] = (steps, need)
        if need is None:
            del needs[chosen]


MARGIN = 5
NOT_YET = (None, (), ())


def decoder_layer(nc, io, out_dram):
    ctx = ExitStack()
    with ctx:
        names = iter(range(10000))

        def sb(name, shape, dt=F32):
            return ctx.enter_context(nc.sbuf_tensor(name, shape, dt))

        def ring(name, n, shape, dt=F32):
            return Ring([sb(f"{name}{i}", shape, dt) for i in range(n)])

        def sig(name):
            return Signal(ctx, nc, "s_" + name)

        banks = Ring([ctx.enter_context(nc.psum_tensor(f"bank{i}", [P, CHUNK], F32)) for i in range(4)])
        b_bank = Ring([ctx.enter_context(nc.psum_tensor("b_bank", [P, CHUNK], F32))])
        down_bank = Ring([ctx.enter_context(nc.psum_tensor("down_bank", [P, CHUNK], F32))])
        y_banks = Ring([ctx.enter_context(nc.psum_tensor("y_banks", [P, BLOCKS, INNER], F32))])

        pe, sync = Queue(sends=200.0, sees=85.0), Queue(sends=2000.0)
        act = Queue(70.0, 0.83, pointer=93.0, sends=100.0, sees=50.0)
        dve = Queue(70.0, 1.04, pointer=60.0, sends=80.0, sees=30.0)
        pool = Queue(150.0, 2.1, sends=30.0, sees=125.0)

        ident = sb("ident", [P, P])
        ident16 = sb("ident16", [P, P], BF16)
        w_in = sb("w_in", [P, 2 * INNER])
        w_xproj = sb("w_xproj", [P, HALVES, DT_RANK + 2 * STATES])
        w_xproj_half = sb("w_xproj_half", [P, HALVES, DT_RANK + 2 * STATES])
        w_dt = sb("w_dt", [DT_RANK, INNER])
        w_out = sb("w_out", [P, HALVES, D])
        conv_w = sb("conv_w", [P, HALVES, TAPS])
        conv_b = sb("conv_b", [P, HALVES])
        b_dt = sb("b_dt", [P, HALVES])
        d_param = sb("d_param", [P, HALVES])
        d_diag = sb("d_diag", [P, HALVES, P])
        a_log = sb("a_log", [P, HALVES, STATES])
        a_exp = sb("a_exp", [P, HALVES, STATES])
        a_neg = sb("a_neg", [P, HALVES, STATES])
        w_q, w_k, w_v = sb("w_q", [P, D]), sb("w_k", [P, D]), sb("w_v", [P, D])
        w_q_swap, w_k_swap = sb("w_q_swap", [P, D]), sb("w_k_swap", [P, D])
        xpos = sb("xpos", [P, 4, T])
        decay_mask = sb("decay_mask", [P, P])
        router_rows = sb("router_rows", [EXPERTS, D])
        w_router = sb("w_router", [P, EXPERTS])
        router_bias = sb("router_bias", [P, EXPERTS])
        expert_no = sb("expert_no", [P, EXPERTS])
        up_w = sb("up_w", [P, EXPERTS, EXPERT_DIM])
        gate_w = sb("gate_w", [P, EXPERTS, EXPERT_DIM])
        down_w = sb("down_w", [P, PAIRS, D])
        shared_rows = sb("shared_rows", [P, 3, P])
        shared_w = sb("shared_w", [P, 3, P])
        pick_bc_rows = sb("pick_bc_rows", [PARTS * 2 * STATES, 2 * STATES])
        pick_bc = sb("pick_bc", [PARTS * 2 * STATES, 2 * STATES, P], BF16)
        pick_expert_rows = sb("pick_expert_rows", [PARTS * EXPERTS, EXPERTS])
        pick_expert = sb("pick_expert", [PARTS * EXPERTS, EXPERTS, EXPERT_DIM], BF16)
        minus_half = sb("minus_half", [P, BLOCKS])

        x_r = ring("x", 2, [P, BLOCKS, D])
        xT_r = ring("xT", 4, [P, CHUNK])
        ctx_r = ring("ctx", 2, [P, BLOCKS, D])
        narrow_r = ring("narrow", 11, [P, CHUNK])
        wide_r = ring("wide", 6, [P, HALVES, CHUNK])
        xc2_r = ring("xc2", 2, [P, HALVES, CHUNK])
        gate_z_r = ring("gate_z", 2, [P, BLOCKS, INNER])
        bc_parts_r = ring("bc_parts", 1, [P, BLOCKS, PARTS, 2 * STATES], BF16)
        bc_rest_r = ring("bc_rest", 1, [P, BLOCKS, 2 * STATES])
        dt_low_r = ring("dt_low", 1, [P, BLOCKS, DT_RANK])
        bcT_r = ring("bcT", 2, [PARTS * 2 * STATES, CHUNK], BF16)
        delta_r = ring("delta", 2, [P, HALVES, CHUNK])
        dx_r = ring("dx", 2, [P, HALVES, CHUNK])

        decay_r = ring("decay", 3, [P, HALVES, CHUNK])
        drive_r = ring("drive", 2, [P, HALVES, CHUNK])
        state_r = ring("state", 2, [P, HALVES, CHUNK])
        c_r = ring("c_all", 3, [P, CHUNK])
        read_r = ring("read", 3, [P, HALVES, CHUNK])

        k_r, v_r = ring("k", 1, [P, CHUNK]), ring("v", 1, [P, CHUNK])
        x2_r = ring("x2", 1, [P, CHUNK])
        stats_r = ring("stats", 3, [P, BLOCKS, 6])
        moments_r = ring("moments", 3, [P, BLOCKS, 2])
        var_eps_r = ring("var_eps", 3, [P, BLOCKS])
        rstd_r = ring("rstd", 3, [P, BLOCKS])
        shift_r = ring("shift", 3, [P, 2, BLOCKS])

        x2T_r = ring("x2T", 2, [P, CHUNK])
        logits_r = ring("logits", 1, [P, BLOCKS, EXPERTS])
        top_r = ring("top", 1, [P, BLOCKS, 8])
        top_at_r = ring("top_at", 1, [P, BLOCKS, 8], U32)
        top_f_r = ring("top_f", 1, [P, BLOCKS, 2])
        soft_r = ring("soft", 1, [P, 4, BLOCKS])
        comb_r = ring("comb", 1, [P, 3, BLOCKS, EXPERTS])
        comb_parts_r = ring("comb_parts", 1, [P, BLOCKS, PARTS, EXPERTS], BF16)
        comb_rest_r = ring("comb_rest", 1, [P, BLOCKS, EXPERTS])
        combT_r = ring("combT", 1, [PARTS * EXPERTS, CHUNK], BF16)
        comb_all_r = ring("comb_all", 2, [P, CHUNK])
        gu_r = ring("gu", 2, [P, CHUNK])
        hid_r = ring("hid", 2, [P, CHUNK])

        s = {n: sig(n) for n in (
            "early_consts", "late_consts", "setup_act", "setup_dve", "setup_pe", "setup_pool",
            "xT_mm", "xT", "xb_mm", "conv_bias", "conv_taps", "z_mm", "z_tanh", "gate_z", "conv_tanh", "xc2",
            "proj_mm", "dt_low", "bc_split", "bcT_mm", "bcT", "dt_lowT_mm", "dt_lowT", "dt_mm", "dt_pre",
            "dt_e", "dt_ln", "dt_dve", "delta", "dx",
            "decay", "c_mm", "c_all", "b_mm", "drive", "state", "read", "y_acc",
            "y_gated", "y_gatedT_mm", "y_gatedT", "out_mm", "stats", "moments", "var_eps", "rstd", "shift", "normed",
            "ctxT_mm", "ctxT", "x1T_mm", "x1T", "q_mm", "q_rot", "q", "k_mm", "k_rot", "k", "v_mm", "v", "score_mm", "ret",
            "retout_mm",
            "x2T_mm", "x2T", "router_mm", "router", "top_exp", "comb_split", "combT_mm", "combT", "comb_mm", "comb_all",
            "gu_mm", "g_tanh", "g_silu", "gu", "hid", "down_mm")}
        for name, count, r in (("x_load", 2, x_r), ("ctx_load", 2, ctx_r)):
            for i in range(count):
                r.free[i].landed = sig(f"{name}{i}")
        s_store = [sig(f"store{i}") for i in range(2)]

        x_view = io["x"].rearrange("b t d -> (b t) d").rearrange("(c q p) d -> c p q d", p=P, q=BLOCKS)
        ctx_view = io["ctx_1024"].rearrange("b t d -> (b t) d").rearrange("(c q p) d -> c p q d", p=P, q=BLOCKS)
        out_view = out_dram.rearrange("b t d -> (b t) d").rearrange("(c q p) d -> c p q d", p=P, q=BLOCKS)

        def load(r, view, c):
            slot = r.take(sync)
            slot.loaded = sync.load(slot.t[:, :, :], view[c], slot.landed)
            return slot

        x_in = {0: load(x_r, x_view, 0)}

        def const(dst, src, signal):
            return sync.load(dst, src, signal)

        def per_channel(dst, vector, signal):
            for h in range(HALVES):
                done = const(dst[:, h:h + 1], vector[h * P:(h + 1) * P].rearrange("(p a) -> p a", a=1), signal)
            return done

        early = s["early_consts"]
        const(ident[:, :], io["c_ident"], early)
        const(w_in[:, :], io["L0_attn_W_in"], early)
        const(conv_w[:, :, :], io["L0_attn_conv_w"].rearrange("(h p) k -> p h k", p=P), early)
        per_channel(conv_b, io["L0_attn_conv_b"], early)
        const(w_xproj[:, :, :], io["L0_attn_W_xproj"].rearrange("(h p) n -> p h n", p=P), early)
        const(w_dt[:, :], io["L0_attn_W_dt"], early)
        per_channel(b_dt, io["L0_attn_b_dt"], early)
        const(a_log[:, :, :], io["L0_attn_A_log"].rearrange("(h p) n -> p h n", p=P), early)
        per_channel(d_param, io["L0_attn_D_param"], early)
        early_in = const(pick_bc_rows[:, :], io["c_pick_bc"], early)
        early_in[0].times[early_in[1]] = 9000.0

        late = s["late_consts"]
        const(xpos[:, :, :], io["c_xpos"], late)
        qkv_slots = [narrow_r.take(sync) for _ in range(3)]
        for slot, name in zip(qkv_slots, ("Wq", "Wk", "Wv")):
            const(slot.t[:, 0:D], io["L0_xattn_" + name], late)
        const(w_out[:, :, :], io["L0_attn_W_out"].rearrange("(h p) n -> p h n", p=P), late)
        const(pick_expert_rows[:, :], io["c_pick_expert"], late)
        const(decay_mask[:, :], io["c_decay_mask"], late)
        const(router_rows[:, :], io["L0_ffn_router_w"], late)
        const(router_bias[:, :], io["L0_ffn_router_bias"].rearrange("(a n) -> a n", a=1).partition_broadcast(P), late)
        const(expert_no[:, :], io["c_expert_no"], late)
        const(shared_rows[:, 0, :], io["L0_ffn_sh_gate"], late)
        const(shared_rows[:, 1, :], io["L0_ffn_sh_up"], late)
        const(shared_rows[:, 2, :], io["L0_ffn_sh_down"], late)
        const(gate_w[:, :, :], io["L0_ffn_gate_proj"].rearrange("k d e -> d k e"), late)
        const(up_w[:, :, :], io["L0_ffn_up_proj"].rearrange("k d e -> d k e"), late)
        late_in = const(down_w[:, :, :], io["L0_ffn_down_proj"].rearrange("k e d -> (k e) d")
                        .rearrange("(j p) d -> p j d", p=P), late)
        late_in[0].times[late_in[1]] = 24000.0

        for slot in decay_r.free:
            zero_decay = pool.fill(slot.whole[:, :, :].rearrange("p h (b t) -> p (h b) t", t=T)[:, :, 0:1], 0.0,
                                   s["setup_pool"])
        pool.fill(minus_half[:, :], -0.5, s["setup_pool"])
        for queue in (act, dve, pool, pe):
            queue.wait(early_in)
        a_exp_done = act.act(a_exp[:, :, :], a_log[:, :, :], ACT.Exp, s["setup_act"])
        dve.ts(w_xproj_half[:, :, :], w_xproj[:, :, :], 0.5, 1.0, ALU.mult, ALU.mult, s["setup_dve"])
        dve.copy(ident16[:, :], ident[:, :], s["setup_dve"])
        for h in range(HALVES):
            dve.ts(d_diag[:, h, :], ident[:, :], d_param[:, h:h + 1], 0.5, ALU.mult, ALU.mult, s["setup_dve"])
        dve.wait(a_exp_done)
        setup_dve = dve.ts(a_neg[:, :, :], a_exp[:, :, :], -1.0, 1.0, ALU.mult, ALU.mult, s["setup_dve"])
        setup_pool = pool.copy(pick_bc[:, :, :],
                               pick_bc_rows[:, :].unsqueeze(2).to_broadcast([PARTS * 2 * STATES, 2 * STATES, P]),
                               s["setup_pool"])

        def seqs(ap):
            return ap.rearrange("p (b t) -> p b t", t=T)

        def blocks(ap):
            return ap.rearrange("p (q n) -> p q n", q=BLOCKS)

        xT_of, prepared, gates = {}, {}, {}
        decays, c_alls, b_alls, drives, states, reads, scanned = {}, {}, {}, {}, {}, {}, {}
        contexts, attended, routed, weights_of, pairs, products, hidden, stores = {}, {}, {}, {}, {}, {}, {}, {}

        ready = {}
        reached = {}

        def got(table, key):
            while key not in table:
                yield NOT_YET
            return table[key]

        def setup():
            yield on(pool, late_in)
            pool.wait(late_in)
            pick_done = pool.copy(
                pick_expert[:, :, :],
                pick_expert_rows[:, :].unsqueeze(2).to_broadcast([PARTS * EXPERTS, EXPERTS, EXPERT_DIM]),
                s["setup_pool"])
            yield on(pe, late_in, takes=(banks,))
            bank = banks.take(pe)
            pe.wait(late_in)
            for i in range(3):
                flipped = pe.transpose(bank.t[:, i * P:(i + 1) * P], qkv_slots[i].t[:, 0:D], ident[:, :],
                                       signal=s["setup_pe"])
            for slot in qkv_slots:
                slot.release(flipped)
            yield on(act, flipped)
            act.wait(flipped)
            for i, w in enumerate((w_q, w_k, w_v)):
                qkv_done = act.act(w[:, :], bank.t[:, i * P:(i + 1) * P], ACT.Copy, s["setup_act"])
            bank.release(qkv_done)
            yield on(dve, qkv_done)
            dve.wait(qkv_done)
            for w, swapped in ((w_q, w_q_swap), (w_k, w_k_swap)):
                from_pairs, to_pairs = (a[:, :].rearrange("p (n two) -> p n two", two=2) for a in (w, swapped))
                for i in (0, 1):
                    swap_done = dve.copy(to_pairs[:, :, i], from_pairs[:, :, 1 - i], s["setup_dve"])
            yield on(pe, takes=(banks,))
            bank = banks.take(pe)
            for i in range(3):
                pe.transpose(bank.t[:, i * P:(i + 1) * P], shared_rows[:, i, :], ident[:, :])
            flipped = pe.transpose(bank.t[:, 3 * P:3 * P + EXPERTS], router_rows[:, :], ident[0:EXPERTS, 0:EXPERTS],
                                   signal=s["setup_pe"])
            yield on(act, flipped)
            act.wait(flipped)
            act.act(shared_w[:, :, :], bank.t[:, 0:3 * P].rearrange("p (i n) -> p i n", i=3), ACT.Copy,
                    s["setup_act"])
            flip_done = act.act(w_router[:, :], bank.t[:, 3 * P:3 * P + EXPERTS], ACT.Copy, s["setup_act"])
            bank.release(flip_done)
            for queue in (pe, dve):
                yield on(queue, late_in, swap_done, flip_done, pick_done)
                queue.wait(late_in, swap_done, flip_done, pick_done)
            ready["weights"] = True

        def prepare():
            for c in range(CHUNKS):
                reached[prepare] = c
                if c + 1 < CHUNKS:
                    yield on(sync, takes=(x_r,))
                    x_in[c + 1] = load(x_r, x_view, c + 1)
                x = x_in.pop(c)
                yield on(pe, x.loaded, takes=(banks,))
                bank = banks.take(pe)
                pe.wait(x.loaded)
                for q in range(BLOCKS):
                    flipped = pe.transpose(bank.t[:, q * P:(q + 1) * P], x.t[:, q, :], ident[:, :],
                                           signal=s["xT_mm"] if q == BLOCKS - 1 else None)
                x.release(flipped)
                yield on(act, flipped, takes=(xT_r,))
                xT = xT_r.take(act)
                act.wait(flipped)
                xT_done = act.act(xT.t[:, :], bank.t[:, :], ACT.Copy, s["xT"])
                bank.release(xT_done)
                xT_of[c] = (xT, xT_done)
                yield on(act, takes=(wide_r,))
                conv = wide_r.take(act)
                for h in range(HALVES):
                    yield on(pe, xT_done, takes=(banks,))
                    bank = banks.take(pe)
                    pe.wait(xT_done)
                    xb_done = pe.matmul(bank.t[:, :], w_in[:, h * P:(h + 1) * P], xT.t[:, :], signal=s["xb_mm"])
                    yield on(act, xb_done)
                    act.wait(xb_done)
                    tap = act.act(conv.t[:, h, :], bank.t[:, :], ACT.Identity, s["conv_bias"],
                                  bias=conv_b[:, h:h + 1], scale=conv_w[:, h, TAPS - 1:TAPS])
                    for k in range(1, TAPS):
                        yield on(dve, tap)
                        dve.wait(tap)
                        late_out = seqs(conv.t[:, h, :])[:, :, k:T]
                        tap = dve.stt(late_out, seqs(bank.t[:, :])[:, :, 0:T - k],
                                      conv_w[:, h, TAPS - 1 - k:TAPS - k], late_out, ALU.mult, ALU.add,
                                      s["conv_taps"])
                    bank.release(tap)
                yield on(act, tap, takes=(wide_r,))
                conv_tanh = wide_r.take(act)
                act.wait(tap)
                tanh_done = act.act(conv_tanh.t[:, :, :], conv.t[:, :, :], ACT.Tanh, s["conv_tanh"], scale=0.5)
                yield on(dve, tanh_done, takes=(xc2_r,))
                xc2 = xc2_r.take(dve)
                dve.wait(tanh_done)
                xc2_done = dve.stt(xc2.t[:, :, :], conv_tanh.t[:, :, :], 1.0, conv.t[:, :, :], ALU.add, ALU.mult,
                                   s["xc2"])
                conv.release(xc2_done)
                conv_tanh.release(xc2_done)
                yield on(pe, xc2_done, takes=(banks,))
                bank = banks.take(pe)
                pe.wait(xc2_done, setup_dve)
                proj_bank = bank
                proj = bank.t[:, 0:BLOCKS * (DT_RANK + 2 * STATES)].rearrange("p (q n) -> p q n", q=BLOCKS)
                for q in range(BLOCKS):
                    for h in range(HALVES):
                        proj_done = pe.matmul(proj[:, q, :], xc2.t[:, h, q * P:(q + 1) * P], w_xproj_half[:, h, :],
                                              start=h == 0, stop=h == HALVES - 1,
                                              signal=s["proj_mm"] if (q, h) == (BLOCKS - 1, HALVES - 1) else None)
                yield on(act, proj_done, takes=(dt_low_r,))
                dt_low = dt_low_r.take(act)
                act.wait(proj_done)
                low_done = act.act(dt_low.t[:, :, :], proj[:, :, 0:DT_RANK], ACT.Copy, s["dt_low"])
                yield on(pe, low_done, takes=(banks,))
                bank = banks.take(pe)
                pe.wait(low_done)
                for q in range(BLOCKS):
                    flipped = pe.transpose(bank.t[0:DT_RANK, q * P:(q + 1) * P], dt_low.t[:, q, :], ident[:, :],
                                           signal=s["dt_lowT_mm"] if q == BLOCKS - 1 else None)
                dt_low.release(flipped)
                yield on(act, flipped, takes=(narrow_r,))
                dt_lowT = narrow_r.take(act)
                act.wait(flipped)
                lowT_done = act.act(dt_lowT.t[0:DT_RANK, :], bank.t[0:DT_RANK, :], ACT.Copy, s["dt_lowT"])
                bank.release(lowT_done)
                yield on(dve, low_done, takes=(bc_parts_r, bc_rest_r))
                parts, rest = bc_parts_r.take(dve), bc_rest_r.take(dve)
                bc = proj[:, :, DT_RANK:]
                dve.wait(low_done)
                done = dve.copy(parts.t[:, :, 0, :], bc, s["bc_split"])
                yield on(dve, done)
                dve.wait(done)
                rest_done = dve.tt(rest.t[:, :, :], bc, parts.t[:, :, 0, :], ALU.subtract, s["bc_split"])
                proj_bank.release(rest_done)
                yield on(dve, rest_done)
                dve.wait(rest_done)
                done = dve.copy(parts.t[:, :, 1, :], rest.t[:, :, :], s["bc_split"])
                yield on(dve, done)
                dve.wait(done)
                split_done = dve.tt(parts.t[:, :, 2, :], rest.t[:, :, :], parts.t[:, :, 1, :], ALU.subtract,
                                    s["bc_split"])
                rest.release(split_done)
                yield on(pe, split_done, takes=(banks,))
                bank = banks.take(pe)
                rows = PARTS * 2 * STATES
                bcT_bank = bank.t[:, :].bitcast(BF16)[0:rows, 0:CHUNK]
                pe.wait(split_done)
                for q in range(BLOCKS):
                    flipped = pe.transpose(bcT_bank[:, q * P:(q + 1) * P],
                                           parts.t[:, q, :, :].rearrange("p a n -> p (a n)"), ident16[:, :],
                                           signal=s["bcT_mm"] if q == BLOCKS - 1 else None)
                parts.release(flipped)
                yield on(act, flipped, takes=(bcT_r,))
                bcT = bcT_r.take(act)
                act.wait(flipped)
                bcT_done = act.act(bcT.t[:, :], bcT_bank, ACT.Copy, s["bcT"])
                bank.release(bcT_done)
                yield on(act, takes=(wide_r, wide_r))
                dt_abs, dt_relu = wide_r.take(act), wide_r.take(act)
                for h in range(HALVES):
                    yield on(pe, lowT_done, takes=(banks,))
                    bank = banks.take(pe)
                    pe.wait(lowT_done)
                    dt_done = pe.matmul(bank.t[:, :], w_dt[:, h * P:(h + 1) * P], dt_lowT.t[0:DT_RANK, :],
                                        signal=s["dt_mm"])
                    yield on(act, dt_done)
                    act.wait(dt_done)
                    act.act(dt_abs.t[:, h, :], bank.t[:, :], ACT.Abs, s["dt_pre"], bias=b_dt[:, h:h + 1])
                    pre_done = act.act(dt_relu.t[:, h, :], bank.t[:, :], ACT.Relu, s["dt_pre"], bias=b_dt[:, h:h + 1])
                    bank.release(pre_done)
                dt_lowT.release(dt_done)
                yield on(act, pre_done, takes=(wide_r,))
                dt_e = wide_r.take(act)
                act.wait(pre_done)
                e_done = act.act(dt_e.t[:, :, :], dt_abs.t[:, :, :], ACT.Exp, s["dt_e"], scale=-1.0)
                yield on(act, e_done)
                act.wait(e_done)
                dt_ln = dt_abs
                ln_done = act.act(dt_ln.t[:, :, :], dt_e.t[:, :, :], ACT.Ln, s["dt_ln"], bias=1.0)
                yield on(dve, e_done, takes=(wide_r,))
                dt_w = wide_r.take(dve)
                dve.wait(e_done)
                done = dve.ts(dt_w.t[:, :, :], dt_e.t[:, :, :], 1.0, -1.0, ALU.add, ALU.add, s["dt_dve"])
                yield on(dve, done)
                dve.wait(done)
                residue = dve.stt(dt_w.t[:, :, :], dt_w.t[:, :, :], -1.0, dt_e.t[:, :, :], ALU.mult, ALU.add,
                                  s["dt_dve"])
                dt_e.release(ln_done, residue)
                yield on(pool, residue, ln_done)
                pool.wait(residue, ln_done)
                log1p = pool.tt(dt_ln.t[:, :, :], dt_ln.t[:, :, :], dt_w.t[:, :, :], ALU.add, s["delta"])
                dt_w.release(log1p)
                yield on(pool, log1p, takes=(delta_r,))
                delta = delta_r.take(pool)
                pool.wait(log1p)
                delta_done = pool.tt(delta.t[:, :, :], dt_ln.t[:, :, :], dt_relu.t[:, :, :], ALU.add, s["delta"])
                dt_ln.release(delta_done)
                dt_relu.release(delta_done)
                yield on(dve, delta_done, takes=(dx_r,))
                dx = dx_r.take(dve)
                dve.wait(delta_done)
                dx_done = dve.stt(dx.t[:, :, :], xc2.t[:, :, :], 0.5, delta.t[:, :, :], ALU.mult, ALU.mult, s["dx"])
                prepared[c] = dict(delta=delta, dx=dx, bcT=bcT, delta_done=delta_done, dx_done=dx_done,
                                   bcT_done=bcT_done, xc2=xc2)

        def gate():
            for c in range(CHUNKS):
                reached[gate] = c
                xT, xT_done = yield from got(xT_of, c)
                yield on(dve, takes=(gate_z_r,))
                gate_z = gate_z_r.take(dve)
                for g in range(2):
                    yield on(pe, xT_done, takes=(banks,))
                    bank = banks.take(pe)
                    pe.wait(xT_done)
                    for q in (0, 1):
                        block = 2 * g + q
                        z_done = pe.matmul(bank.t[:, q * INNER:(q + 1) * INNER], xT.t[:, block * P:(block + 1) * P],
                                           w_in[:, INNER:2 * INNER], signal=s["z_mm"] if q else None)
                    yield on(act, z_done, takes=(narrow_r,))
                    z_tanh = narrow_r.take(act)
                    act.wait(z_done)
                    tanh_done = act.act(z_tanh.t[:, :], bank.t[:, :], ACT.Tanh, s["z_tanh"], scale=0.5)
                    yield on(dve, tanh_done)
                    dve.wait(tanh_done)
                    gate_done = dve.stt(gate_z.t[:, 2 * g:2 * g + 2, :].rearrange("p q n -> p (q n)"),
                                        z_tanh.t[:, :], 1.0, bank.t[:, :], ALU.add, ALU.mult, s["gate_z"])
                    bank.release(gate_done)
                    z_tanh.release(gate_done)
                gates[c] = (gate_z, gate_done)

        STEPS = CHUNKS * STATES

        def decay():
            act.wait(setup_dve, zero_decay)
            for k in range(STEPS):
                reached[decay] = k / STATES
                c, n = divmod(k, STATES)
                p = yield from got(prepared, c)
                yield on(act, p["delta_done"], takes=(decay_r,))
                slot = decay_r.take(act)
                act.wait(p["delta_done"])
                for h in range(HALVES):
                    done = act.act(seqs(slot.t[:, h, :])[:, :, 1:T], seqs(p["delta"].t[:, h, :])[:, :, 1:T], ACT.Exp,
                                   s["decay"], scale=a_neg[:, h, n:n + 1])
                decays[k] = (slot, done)
                if n == STATES - 1:
                    p["delta"].release(done, p["dx_done"])

        def spread_c():
            yield on(pe, setup_pool)
            pe.wait(setup_pool)
            for k in range(STEPS):
                reached[spread_c] = k / STATES
                c, n = divmod(k, STATES)
                p = yield from got(prepared, c)
                yield on(pe, p["bcT_done"], takes=(banks, c_r))
                bank = banks.take(pe)
                slot = c_r.take(act)
                pe.wait(p["bcT_done"])
                c_mm = pe.matmul(bank.t[:, :], pick_bc[:, STATES + n, :], p["bcT"].t[:, :], signal=s["c_mm"])
                yield on(act, c_mm)
                act.wait(c_mm)
                copied = act.act(slot.t[:, :], bank.t[:, :], ACT.Copy, s["c_all"])
                bank.release(copied)
                c_alls[k] = (slot, copied)
                if n == STATES - 1:
                    p["c_spread"] = c_mm

        def spread_b():
            yield on(pe, setup_pool)
            pe.wait(setup_pool)
            for k in range(STEPS):
                reached[spread_b] = k / STATES
                c, n = divmod(k, STATES)
                p = yield from got(prepared, c)
                yield on(pe, p["bcT_done"], takes=(b_bank,))
                bank = b_bank.take(pe)
                pe.wait(p["bcT_done"])
                done = pe.matmul(bank.t[:, :], pick_bc[:, n, :], p["bcT"].t[:, :], signal=s["b_mm"])
                b_alls[k] = (bank, done)
                if n == STATES - 1:
                    c_mm = yield from got(p, "c_spread")
                    p["bcT"].release(done, c_mm)

        def drive():
            for k in range(STEPS):
                reached[drive] = k / STATES
                c, n = divmod(k, STATES)
                bank, spread = yield from got(b_alls, k)
                p = prepared[c]
                yield on(dve, p["dx_done"], spread, takes=(drive_r,))
                slot = drive_r.take(dve)
                dve.wait(p["dx_done"], spread)
                done = dve.tt(slot.t[:, :, :], p["dx"].t[:, :, :],
                              bank.t[:, :].unsqueeze(1).to_broadcast([P, HALVES, CHUNK]), ALU.mult, s["drive"])
                bank.release(done)
                drives[k] = (slot, done)
                if n == STATES - 1:
                    p["dx"].release(done)

        def scan():
            flat = "p h n -> p (h n)"
            for k in range(STEPS):
                reached[scan] = k / STATES
                decay_slot, decay_done = yield from got(decays, k)
                drive_slot, drive_done = yield from got(drives, k)
                yield on(dve, decay_done, drive_done, takes=(state_r,))
                slot = state_r.take(dve)
                dve.wait(decay_done, drive_done)
                done = dve.scan(*(x.t[:, :, :].rearrange(flat) for x in (slot, decay_slot, drive_slot)), s["state"])
                decay_slot.release(done)
                drive_slot.release(done)
                states[k] = (slot, done)

        def read():
            for k in range(STEPS):
                reached[read] = k / STATES
                state, scan_done = yield from got(states, k)
                c_all, copied = yield from got(c_alls, k)
                yield on(pool, scan_done, copied, takes=(read_r,))
                slot = read_r.take(pool)
                pool.wait(scan_done, copied)
                done = pool.tt(slot.t[:, :, :], state.t[:, :, :],
                               c_all.t[:, :].unsqueeze(1).to_broadcast([P, HALVES, CHUNK]), ALU.mult, s["read"])
                state.release(done)
                c_all.release(done)
                reads[k] = (slot, done)

        def sum_states():
            for k in range(STEPS):
                reached[sum_states] = k / STATES
                c, n = divmod(k, STATES)
                slot, read_done = yield from got(reads, k)
                if n == 0:
                    yield on(pe, read_done, takes=(y_banks,))
                    y = y_banks.take(pe)
                else:
                    yield on(pe, read_done)
                pe.wait(read_done)
                for q in range(BLOCKS):
                    for h in range(HALVES):
                        done = pe.transpose(y.t[:, q, h * P:(h + 1) * P], slot.t[:, h, q * P:(q + 1) * P],
                                            ident[:, :], start=(n == 0 and h == 0 and q % 2 == 0), stop=False,
                                            signal=s["y_acc"] if (q, h) == (BLOCKS - 1, HALVES - 1) else None)
                slot.release(done)
                if n == STATES - 1:
                    p = prepared[c]
                    for q in range(BLOCKS):
                        for h in range(HALVES):
                            done = pe.matmul(y.t[:, q, h * P:(h + 1) * P], p["xc2"].t[:, h, q * P:(q + 1) * P],
                                             d_diag[:, h, :], start=False,
                                             signal=s["y_acc"] if (q, h) == (BLOCKS - 1, HALVES - 1) else None)
                    p["xc2"].release(done, p["dx_done"])
                    scanned[c] = (y, done)

        def normalise(bank, sum_done, out_ring):
            total = blocks(bank.t[:, :])
            yield on(dve, sum_done, takes=(stats_r, moments_r))
            stats, moments = stats_r.take(dve), moments_r.take(dve)
            dve.wait(sum_done)
            for q in range(BLOCKS):
                stats_done = dve.bn_stats(stats.t[:, q, :], total[:, q, :], s["stats"])
            yield on(dve, stats_done)
            dve.wait(stats_done)
            for q in range(BLOCKS):
                done = dve.bn_aggr(moments.t[:, q, :], stats.t[:, q, :], s["moments"])
            stats.release(done)
            yield on(pool, done, takes=(shift_r, var_eps_r, rstd_r))
            shift, var_eps, rstd = shift_r.take(pool), var_eps_r.take(pool), rstd_r.take(pool)
            pool.wait(done)
            eps_done = pool.ts(var_eps.t[:, :], moments.t[:, :, 1], LN_EPS, 1.0, ALU.add, ALU.mult, s["var_eps"])
            less_mean = pool.ts(shift.t[:, 0, :], moments.t[:, :, 0], -1.0, 1.0, ALU.mult, ALU.mult, s["shift"])
            moments.release(eps_done, less_mean)
            pool.wait(eps_done)
            rstd_done = pool.tt(rstd.t[:, :], var_eps.t[:, :], minus_half[:, :], ALU.pow, s["rstd"])
            var_eps.release(rstd_done)
            pool.wait(rstd_done, less_mean)
            shift_done = pool.tt(shift.t[:, 1, :], shift.t[:, 0, :], rstd.t[:, :], ALU.mult, s["shift"])
            yield on(act, shift_done, stats_done, takes=(out_ring,))
            out = out_ring.take(act, blocks=True)
            act.wait(shift_done)
            act.wait(stats_done)
            for q in range(BLOCKS):
                done = act.act(out.t[:, q, :], total[:, q, :], ACT.Identity, s["normed"],
                               bias=shift.t[:, 1, q:q + 1], scale=rstd.t[:, q:q + 1])
            bank.release(done)
            shift.release(done)
            rstd.release(done)
            return out, done

        def to_channels(src, src_done, bank_ring, out_ring, mm_signal, signal):
            yield on(pe, src_done, takes=(bank_ring,))
            bank = bank_ring.take(pe)
            pe.wait(src_done)
            for q in range(BLOCKS):
                flipped = pe.transpose(bank.t[:, q * P:(q + 1) * P], src[:, q, :], ident[:, :],
                                       signal=mm_signal if q == BLOCKS - 1 else None)
            yield on(act, flipped, takes=(out_ring,))
            out = out_ring.take(act)
            act.wait(flipped)
            copied = act.act(out.t[:, :], bank.t[:, :], ACT.Copy, signal)
            bank.release(copied)
            return out, flipped, copied

        def rotate(w, w_swap, src, src_done, table, out_ring, name):
            turned = []
            for i, weights in enumerate((w, w_swap)):
                yield on(pe, src_done, takes=(banks,))
                bank = banks.take(pe)
                pe.wait(src_done)
                mm_done = pe.matmul(bank.t[:, :], weights[:, :], src[:, :], signal=s[name + "_mm"])
                yield on(dve, mm_done, takes=(narrow_r,))
                rot = narrow_r.take(dve)
                dve.wait(mm_done)
                done = dve.tt(seqs(rot.t[:, :]), seqs(bank.t[:, :]),
                              xpos[:, 2 * table + i, :].unsqueeze(1).to_broadcast([P, CHUNK_SEQS, T]), ALU.mult,
                              s[name + "_rot"])
                bank.release(done)
                turned.append(rot)
            yield on(pool, done, takes=(out_ring,))
            out = out_ring.take(pool)
            pool.wait(done)
            added = pool.tt(out.t[:, :], turned[0].t[:, :], turned[1].t[:, :], ALU.add, s[name])
            for rot in turned:
                rot.release(added)
            return out, added, mm_done

        def context():
            yield from got(ready, "weights")
            for c in range(CHUNKS):
                reached[context] = c
                yield on(sync, takes=(ctx_r,))
                slot = load(ctx_r, ctx_view, c)
                ctxT, ctx_mm, ctxT_done = yield from to_channels(slot.t, slot.loaded, banks, narrow_r, s["ctxT_mm"],
                                                                 s["ctxT"])
                slot.release(ctx_mm)
                k_t, k_done, mm = yield from rotate(w_k, w_k_swap, ctxT.t, ctxT_done, 1, k_r, "k")
                yield on(pe, takes=(banks,))
                bank = banks.take(pe)
                for q in range(BLOCKS):
                    mm = pe.matmul(bank.t[:, q * P:(q + 1) * P], ctxT.t[:, q * P:(q + 1) * P], w_v[:, :],
                                   signal=s["v_mm"] if q == BLOCKS - 1 else None)
                ctxT.release(mm)
                yield on(act, mm, takes=(v_r,))
                v = v_r.take(act, blocks=True)
                act.wait(mm)
                v_done = act.act(v.t[:, :, :], blocks(bank.t[:, :]), ACT.Copy, s["v"])
                bank.release(v_done)
                contexts[c] = (k_t, k_done, v, v_done)

        def attend():
            yield from got(ready, "weights")
            for c in range(CHUNKS):
                reached[attend] = c
                y, y_done = yield from got(scanned, c)
                gate_z, gate_done = yield from got(gates, c)
                yield on(dve, y_done, gate_done, takes=(wide_r,))
                y_gated = wide_r.take(dve)
                gated_y = y_gated.t[:, :, :].rearrange("p h n -> p (h n)").rearrange("p (q n) -> p q n", q=BLOCKS)
                dve.wait(y_done, gate_done)
                for g in range(2):
                    half = slice(2 * g, 2 * g + 2)
                    gated = dve.stt(gated_y[:, half, :], gate_z.t[:, half, :], 0.5, y.t[:, half, :], ALU.mult,
                                    ALU.mult, s["y_gated"])
                y.release(gated)
                gate_z.release(gated)
                yield on(act, takes=(wide_r,))
                y_gatedT = wide_r.take(act)
                for h in range(HALVES):
                    yield on(pe, gated, takes=(banks,))
                    bank = banks.take(pe)
                    pe.wait(gated)
                    for q in range(BLOCKS):
                        flipped = pe.transpose(bank.t[:, q * P:(q + 1) * P], gated_y[:, q, h * P:(h + 1) * P],
                                               ident[:, :], signal=s["y_gatedT_mm"] if q == BLOCKS - 1 else None)
                    yield on(act, flipped)
                    act.wait(flipped)
                    copied = act.act(y_gatedT.t[:, h, :], bank.t[:, :], ACT.Copy, s["y_gatedT"])
                    bank.release(copied)
                y_gated.release(flipped)
                yield on(pe, copied, takes=(banks,))
                bank = banks.take(pe)
                pe.wait(copied)
                xT, xT_done = xT_of.pop(c)
                for q in range(BLOCKS):
                    cols = slice(q * P, (q + 1) * P)
                    pe.transpose(bank.t[:, cols], xT.t[:, cols], ident[:, :], start=True, stop=False)
                    for h in range(HALVES):
                        mm = pe.matmul(bank.t[:, cols], y_gatedT.t[:, h, cols], w_out[:, h, :], start=False,
                                       stop=h == HALVES - 1,
                                       signal=s["out_mm"] if (q, h) == (BLOCKS - 1, HALVES - 1) else None)
                y_gatedT.release(mm)
                xT.release(mm)
                x1, x1_done = yield from normalise(bank, mm, narrow_r)
                x1T, x1T_mm, x1T_done = yield from to_channels(x1.t, x1_done, banks, narrow_r, s["x1T_mm"], s["x1T"])
                x1.release(x1T_mm)
                q_t, q_done, mm = yield from rotate(w_q, w_q_swap, x1T.t, x1T_done, 0, narrow_r, "q")
                k_t, k_done, v, v_done = yield from got(contexts, c)
                yield on(pe, q_done, k_done, takes=(banks,))
                bank = banks.take(pe)
                pe.wait(q_done, k_done)
                for q in range(BLOCKS):
                    cols = slice(q * P, (q + 1) * P)
                    mm = pe.matmul(bank.t[:, cols], k_t.t[:, cols], q_t.t[:, cols],
                                   signal=s["score_mm"] if q == BLOCKS - 1 else None)
                k_t.release(mm)
                q_t.release(mm)
                yield on(dve, mm, takes=(narrow_r,))
                ret = narrow_r.take(dve, blocks=True)
                dve.wait(mm)
                ret_done = dve.tt(ret.t[:, :, :], blocks(bank.t[:, :]),
                                  decay_mask[:, :].unsqueeze(1).to_broadcast([P, BLOCKS, P]), ALU.mult, s["ret"])
                bank.release(ret_done)
                yield on(pe, ret_done, v_done, takes=(banks,))
                bank = banks.take(pe)
                pe.wait(ret_done, v_done)
                for q in range(BLOCKS):
                    cols = slice(q * P, (q + 1) * P)
                    pe.transpose(bank.t[:, cols], x1T.t[:, cols], ident[:, :], start=True, stop=False)
                    mm = pe.matmul(bank.t[:, cols], ret.t[:, q, :], v.t[:, q, :], start=False,
                                   signal=s["retout_mm"] if q == BLOCKS - 1 else None)
                ret.release(mm)
                v.release(mm)
                x1T.release(mm)
                attended[c] = yield from normalise(bank, mm, x2_r)

        def route():
            for c in range(CHUNKS):
                reached[route] = c
                x2, x2_done = yield from got(attended, c)
                x2T, x2T_mm, x2T_done = yield from to_channels(x2.t, x2_done, banks, x2T_r, s["x2T_mm"], s["x2T"])
                x2.release(x2T_mm)
                yield on(pe, x2T_done, takes=(banks,))
                bank = banks.take(pe)
                pe.wait(x2T_done)
                scores = bank.t[:, 0:BLOCKS * EXPERTS].rearrange("p (q n) -> p q n", q=BLOCKS)
                for q in range(BLOCKS):
                    mm = pe.matmul(scores[:, q, :], x2T.t[:, q * P:(q + 1) * P], w_router[:, :],
                                   signal=s["router_mm"] if q == BLOCKS - 1 else None)
                routed[c] = (x2T, x2T_done)
                shape = [P, BLOCKS, EXPERTS]
                yield on(dve, mm, takes=(logits_r,))
                logits = logits_r.take(dve)
                dve.wait(mm)
                done = dve.tt(logits.t[:, :, :], scores, router_bias[:, :].unsqueeze(1).to_broadcast(shape), ALU.add,
                              s["router"])
                bank.release(done)
                yield on(dve, done, takes=(top_r, top_at_r))
                top, top_at = top_r.take(dve), top_at_r.take(dve)
                dve.wait(done)
                for q in range(BLOCKS):
                    done = dve.max8(top.t[:, q, :], logits.t[:, q, :], s["router"])
                yield on(dve, done)
                dve.wait(done)
                for q in range(BLOCKS):
                    at_done = dve.max8_index(top_at.t[:, q, :], top.t[:, q, :], logits.t[:, q, :], s["router"])
                logits.release(at_done)
                yield on(dve, at_done, takes=(soft_r, top_f_r))
                soft, top_f = soft_r.take(dve), top_f_r.take(dve)
                dve.wait(at_done)
                done = dve.tt(soft.t[:, 0, :], top.t[:, :, 1], top.t[:, :, 0], ALU.subtract, s["router"])
                f_done = dve.copy(top_f.t[:, :, :], top_at.t[:, :, 0:2], s["router"])
                top.release(done)
                top_at.release(f_done)
                yield on(act, done)
                act.wait(done)
                e_done = act.act(soft.t[:, 1, :], soft.t[:, 0, :], ACT.Exp, s["top_exp"])
                yield on(dve, e_done)
                dve.wait(e_done)
                done = dve.ts(soft.t[:, 0, :], soft.t[:, 1, :], 1.0, 1.0, ALU.add, ALU.mult, s["router"])
                yield on(dve, done)
                dve.wait(done)
                done = dve.reciprocal(soft.t[:, 2, :], soft.t[:, 0, :], s["router"])
                yield on(dve, done)
                dve.wait(done)
                p2_done = dve.tt(soft.t[:, 3, :], soft.t[:, 1, :], soft.t[:, 2, :], ALU.mult, s["router"])
                yield on(dve, f_done, takes=(comb_r,))
                comb = comb_r.take(dve)
                dve.wait(f_done)
                for i in (0, 1):
                    eq = dve.tt(comb.t[:, i, :, :], expert_no[:, :].unsqueeze(1).to_broadcast(shape),
                                top_f.t[:, :, i].unsqueeze(2).to_broadcast(shape), ALU.is_equal, s["router"])
                yield on(dve, eq, p2_done)
                dve.wait(eq, p2_done)
                for i in (0, 1):
                    done = dve.tt(comb.t[:, i, :, :], comb.t[:, i, :, :],
                                  soft.t[:, 2 + i, :].unsqueeze(2).to_broadcast(shape), ALU.mult, s["router"])
                top_f.release(eq)
                soft.release(done)
                yield on(dve, done)
                dve.wait(done)
                done = dve.tt(comb.t[:, 2, :, :], comb.t[:, 0, :, :], comb.t[:, 1, :, :], ALU.add, s["router"])
                yield on(dve, done, takes=(comb_parts_r, comb_rest_r))
                parts, rest = comb_parts_r.take(dve), comb_rest_r.take(dve)
                whole = comb.t[:, 2, :, :]
                dve.wait(done)
                done = dve.copy(parts.t[:, :, 0, :], whole, s["comb_split"])
                yield on(dve, done)
                dve.wait(done)
                done = dve.tt(rest.t[:, :, :], whole, parts.t[:, :, 0, :], ALU.subtract, s["comb_split"])
                comb.release(done)
                yield on(dve, done)
                dve.wait(done)
                done = dve.copy(parts.t[:, :, 1, :], rest.t[:, :, :], s["comb_split"])
                yield on(dve, done)
                dve.wait(done)
                split_done = dve.tt(parts.t[:, :, 2, :], rest.t[:, :, :], parts.t[:, :, 1, :], ALU.subtract,
                                    s["comb_split"])
                rest.release(split_done)
                yield on(pe, split_done, takes=(banks,))
                bank = banks.take(pe)
                rows = PARTS * EXPERTS
                combT_bank = bank.t[:, :].bitcast(BF16)[0:rows, 0:CHUNK]
                pe.wait(split_done)
                for q in range(BLOCKS):
                    mm = pe.transpose(combT_bank[:, q * P:(q + 1) * P],
                                      parts.t[:, q, :, :].rearrange("p a n -> p (a n)"), ident16[:, :],
                                      signal=s["combT_mm"] if q == BLOCKS - 1 else None)
                parts.release(mm)
                yield on(act, mm, takes=(combT_r,))
                combT = combT_r.take(act)
                act.wait(mm)
                combT_done = act.act(combT.t[:, :], combT_bank, ACT.Copy, s["combT"])
                bank.release(combT_done)
                for j in range(PAIRS):
                    reached[route] = c + (j + 1) / len(TILES)
                    yield on(pe, combT_done, takes=(banks, comb_all_r))
                    bank = banks.take(pe)
                    slot = comb_all_r.take(act)
                    pe.wait(combT_done)
                    mm = pe.matmul(bank.t[:, :], pick_expert[:, 2 * j:2 * j + 2, :].rearrange("p k e -> p (k e)"),
                                   combT.t[:, :], signal=s["comb_mm"])
                    yield on(act, mm)
                    act.wait(mm)
                    copied = act.act(slot.t[:, :], bank.t[:, :], ACT.Copy, s["comb_all"])
                    bank.release(copied)
                    weights_of[c, j] = (slot, copied)
                combT.release(mm)

        TILES = [None] + list(range(PAIRS))

        def up_gate():
            for c in range(CHUNKS):
                x2T, x2T_done = yield from got(routed, c)
                for j in TILES:
                    reached[up_gate] = c + (0 if j is None else j + 1) / len(TILES)
                    yield on(pe, x2T_done, takes=(banks, banks))
                    pe.wait(x2T_done)
                    pair = []
                    for i, w in enumerate((gate_w, up_w)):
                        lhsT = (shared_w[:, i, :] if j is None else
                                w[:, 2 * j:2 * j + 2, :].rearrange("p k e -> p (k e)"))
                        bank = banks.take(pe)
                        pair.append((bank, pe.matmul(bank.t[:, :], lhsT, x2T.t[:, :], signal=s["gu_mm"])))
                    pairs[c, j] = pair

        def activate():
            for c in range(CHUNKS):
                for j in TILES:
                    reached[activate] = c + (0 if j is None else j + 1) / len(TILES)
                    (g_bank, g_mm), (u_bank, u_mm) = yield from got(pairs, (c, j))
                    yield on(act, g_mm, takes=(narrow_r,))
                    g_tanh = narrow_r.take(act)
                    act.wait(g_mm)
                    tanh_done = act.act(g_tanh.t[:, :], g_bank.t[:, :], ACT.Tanh, s["g_tanh"], scale=0.5)
                    yield on(dve, tanh_done, takes=(narrow_r,))
                    g_silu = narrow_r.take(dve)
                    dve.wait(tanh_done)
                    silu_done = dve.stt(g_silu.t[:, :], g_tanh.t[:, :], 1.0, g_bank.t[:, :], ALU.add, ALU.mult,
                                        s["g_silu"])
                    g_bank.release(silu_done)
                    g_tanh.release(silu_done)
                    target_ring = hid_r if j is None else gu_r
                    yield on(dve, silu_done, u_mm, takes=(target_ring,))
                    target = target_ring.take(dve)
                    dve.wait(silu_done, u_mm)
                    done = dve.stt(target.t[:, :], g_silu.t[:, :], 0.5, u_bank.t[:, :], ALU.mult, ALU.mult, s["gu"])
                    u_bank.release(done)
                    g_silu.release(done)
                    (hidden if j is None else products)[c, j] = (target, done)

        def weigh():
            for c in range(CHUNKS):
                for j in range(PAIRS):
                    reached[weigh] = c + (j + 1) / len(TILES)
                    product, product_done = yield from got(products, (c, j))
                    weight, weight_done = yield from got(weights_of, (c, j))
                    yield on(pool, product_done, weight_done, takes=(hid_r,))
                    hid = hid_r.take(pool)
                    pool.wait(product_done, weight_done)
                    done = pool.tt(hid.t[:, :], product.t[:, :], weight.t[:, :], ALU.mult, s["hid"])
                    product.release(done)
                    weight.release(done)
                    hidden[c, j] = (hid, done)

        def down():
            for c in range(CHUNKS):
                for j in TILES:
                    reached[down] = c + (0 if j is None else j + 1) / len(TILES)
                    hid, hid_done = yield from got(hidden, (c, j))
                    x2T = routed[c][0]
                    if j is None:
                        yield on(pe, hid_done, takes=(down_bank,))
                        bank = down_bank.take(pe)
                    else:
                        yield on(pe, hid_done)
                    pe.wait(hid_done)
                    w = shared_w[:, 2, :] if j is None else down_w[:, j, :]
                    for q in range(BLOCKS):
                        cols = slice(q * P, (q + 1) * P)
                        if j is None:
                            pe.transpose(bank.t[:, cols], x2T.t[:, cols], ident[:, :], start=q == 0, stop=False)
                        mm = pe.matmul(bank.t[:, cols], hid.t[:, cols], w, start=False, stop=j == PAIRS - 1,
                                       signal=s["down_mm"] if q == BLOCKS - 1 else None)
                    hid.release(mm)
                x2T.release(mm)
                y, y_done = yield from normalise(bank, mm, narrow_r)
                yield on(sync, y_done)
                sync.wait(y_done)
                stored = sync.load(out_view[c], y.t[:, :, :], s_store[c % 2])
                y.release(stored)
                stores[c % 2] = stored

        run({
            setup: -1.5, prepare: -1, attend: 1, route: 1.2, gate: 0, scan: 0, drive: 0,
            read: -0.197, decay: 0, spread_b: 0, spread_c: 0, sum_states: 0, down: 2.021,
            activate: 1.867, up_gate: 2.069, weigh: 1.921, context: 0.5}, reached)
        sync.wait(*stores.values())

        block = ctx.enter_context(nc.Block())

        @block.sync
        def _(eng):
            sync.emit(eng)

        @block.tensor
        def _(eng):
            pe.emit(eng)

        @block.scalar
        def _(eng):
            act.emit(eng)

        @block.vector
        def _(eng):
            dve.emit(eng)

        @block.gpsimd
        def _(eng):
            pool.emit(eng)


def shape_constants(np):
    f = np.float32
    pos = np.arange(T, dtype=np.float64)
    base = (np.arange(0, D, 2, dtype=np.float64) + 0.4 * D) / (1.4 * D)
    freqs = 1.0 / 10000.0 ** (np.arange(D // 2, dtype=np.float64) / (D // 2))
    scale = base[:, None] ** (pos[None, :] / 512.0)
    angle = freqs[:, None] * pos[None, :]
    sign = np.where(np.arange(D) % 2 == 0, -1.0, 1.0)[:, None]
    tables = []
    for factor in (scale, 1.0 / scale):
        tables += [np.repeat(np.cos(angle) * factor, 2, axis=0), np.repeat(np.sin(angle) * factor, 2, axis=0) * sign]
    key, query = np.arange(P)[:, None], np.arange(P)[None, :]
    mask = np.where((key // T == query // T) & (query >= key), 0.96875 ** np.maximum(query - key, 0.0), 0.0)

    def picks(n):
        return (np.arange(PARTS * n)[:, None] % n == np.arange(n)[None, :]).astype(f)

    return {
        "c_ident": np.eye(P, dtype=f),
        "c_xpos": np.ascontiguousarray(np.stack(tables, axis=1)).astype(f),
        "c_decay_mask": mask.astype(f),
        "c_pick_bc": picks(2 * STATES),
        "c_pick_expert": picks(EXPERTS),
        "c_expert_no": np.tile(np.arange(EXPERTS, dtype=f), (P, 1)),
    }


def kernel(**inputs):
    import numpy as _np
    import concourse.bacc as _bacc
    from concourse import mybir as _mybir
    from concourse.bass_utils import run_bass_kernel_spmd as _run

    nc = _bacc.Bacc("TRN2", target_bir_lowering=False, num_devices=1)
    arrays, io = {}, {}
    given = {n: _np.ascontiguousarray(a) for n, a in inputs.items()}
    for name, a in list(given.items()) + list(shape_constants(_np).items()):
        arrays[f"in_{name}_dram"] = a
        io[name] = nc.dram_tensor(f"in_{name}_dram", a.shape, _mybir.dt.from_np(a.dtype), kind="ExternalInput").ap()
    out = nc.dram_tensor("out_0_dram", (SEQS, T, D), F32, kind="ExternalOutput").ap()
    decoder_layer(nc, io, out)
    r = _run(nc, [arrays], core_ids=[0])
    return r.results[0]["out_0_dram"]
```
